# Optimizing a Trainium2 kernel written in Bass

```python
import numpy as np
import jax
import jax.numpy as jnp

def _softmax(x, axis=-1):
    return jax.nn.softmax(x, axis=axis)

def _gelu(x):
    return jax.nn.gelu(x, approximate=True)

def _silu(x):
    return jax.nn.silu(x)

def _sigmoid(x):
    return jax.nn.sigmoid(x)

def _layernorm(x, axis=-1, eps=1e-05):
    m = jnp.mean(x, axis=axis, keepdims=True)
    v = jnp.var(x, axis=axis, keepdims=True)
    return (x - m) / jnp.sqrt(v + eps)

def _scatter_add(tgt, idx, src, axis=0):
    return tgt.at[idx].add(src)

def _segment_sum(src, seg, n):
    return jax.ops.segment_sum(src, seg, n)
kernel_name = 'mk_cond_seq_d2_seqx_r2_3e7d89'

def setup_inputs(seed: int=0):
    np.random.seed(seed)
    _w = jnp.asarray

    def _rec_inputs():
        import jax
        import jax.numpy as jnp
        _rk = jax.random.key(seed)
        x = -0.0002928 + 1 * jax.random.normal(jax.random.fold_in(_rk, 1), (2, 2048, 512), jnp.float32)
        _lenS = 2048 - jax.random.randint(jax.random.fold_in(_rk, 7), (2,), 0, max(1, 2048 // 4) + 1, jnp.int32)
        _lenS2 = 2048 - jax.random.randint(jax.random.fold_in(_rk, 8), (2,), 0, max(1, 2048 // 4) + 1, jnp.int32)
        itok_B_0_7 = jax.random.randint(jax.random.fold_in(_rk, 11), (2,), 0, 8, jnp.int32)
        condB_theta = jax.random.uniform(jax.random.fold_in(_rk, 12), (2,), jnp.float32, 0.0, 0.983423)
        condB_phi = jax.random.uniform(jax.random.fold_in(_rk, 13), (2,), jnp.float32, 0.0, 0.961312)
        return (x, itok_B_0_7, condB_theta, condB_phi)
    x, itok_B_0_7, condB_theta, condB_phi = _rec_inputs()

    def _L0_cond_setup():
        import jax, jax.numpy as jnp
        import numpy as np
        E, H, I = (8, 512, 2048)
        B, S = (4, 512)
        LN_EPS = 1e-12
        key = jax.random.key(seed)
        ks = jax.random.split(key, 8)
        x = jax.random.normal(ks[0], (B, S, H), dtype=jnp.float32)
        expert_idx = jax.random.randint(ks[1], (B,), 0, E, dtype=jnp.int64)
        Wi = jax.random.normal(ks[2], (E, H, I), dtype=jnp.float32) * 0.02
        bi = jnp.zeros((E, I), dtype=jnp.float32)
        Wo = jax.random.normal(ks[3], (E, I, H), dtype=jnp.float32) * 0.02
        bo = jnp.zeros((E, H), dtype=jnp.float32)
        gamma = jnp.ones((E, H), dtype=jnp.float32)
        beta = jnp.zeros((E, H), dtype=jnp.float32)
        return {'input_tensor': x, 'expert_idx': expert_idx, 'Wi': Wi, 'bi': bi, 'Wo': Wo, 'bo': bo, 'gamma': gamma, 'beta': beta}
    _L0_cond_all = _L0_cond_setup()
    _L0_cond_in = {k: v for k, v in _L0_cond_all.items() if k in ('Wi', 'bi', 'Wo', 'bo', 'gamma', 'beta')}
    del _L0_cond_all

    def _L1_cond_setup():
        import jax, jax.numpy as jnp
        import numpy as np
        key = jax.random.key(seed)
        k1, k2, k3 = jax.random.split(key, 3)
        B, N, D = (16, 2048, 512)
        embeddings = jax.random.normal(k1, (B, N, D), dtype=jnp.float32)
        theta = jax.random.uniform(k2, (B,), dtype=jnp.float32)
        phi = jax.random.uniform(k3, (B,), dtype=jnp.float32)
        return {'embeddings': embeddings, 'theta': theta, 'phi': phi}
    _L1_cond_all = _L1_cond_setup()
    _L1_cond_in = {k: v for k, v in _L1_cond_all.items() if k in ()}
    del _L1_cond_all
    return {'x': x, 'itok_B_0_7': itok_B_0_7, 'condB_theta': condB_theta, 'condB_phi': condB_phi, 'L0_cond_Wi': _L0_cond_in['Wi'], 'L0_cond_bi': _L0_cond_in['bi'], 'L0_cond_Wo': _L0_cond_in['Wo'], 'L0_cond_bo': _L0_cond_in['bo'], 'L0_cond_gamma': _L0_cond_in['gamma'], 'L0_cond_beta': _L0_cond_in['beta']}

def reference(x, itok_B_0_7, condB_theta, condB_phi, L0_cond_Wi, L0_cond_bi, L0_cond_Wo, L0_cond_bo, L0_cond_gamma, L0_cond_beta):
    import jax
    import jax.numpy as jnp

    def _L0_cond_ref(input_tensor, expert_idx, Wi, bi, Wo, bo, gamma, beta):
        import jax, jax.numpy as jnp
        import numpy as np
        E, H, I = (8, 512, 2048)
        B, S = (4, 512)
        LN_EPS = 1e-12
        Wi_b = Wi[expert_idx]
        bi_b = bi[expert_idx]
        Wo_b = Wo[expert_idx]
        bo_b = bo[expert_idx]
        g_b = gamma[expert_idx]
        be_b = beta[expert_idx]
        h = jax.nn.gelu(jnp.einsum('bsh,bhi->bsi', input_tensor, Wi_b) + bi_b[:, None, :], approximate=False)
        o = jnp.einsum('bsi,bih->bsh', h, Wo_b) + bo_b[:, None, :]
        r = o + input_tensor
        mu = jnp.mean(r, axis=-1, keepdims=True)
        var = jnp.mean(jnp.square(r - mu), axis=-1, keepdims=True)
        y = (r - mu) * jax.lax.rsqrt(var + LN_EPS)
        return y * g_b[:, None, :] + be_b[:, None, :]

    def _L1_cond_ref(embeddings, theta, phi):
        import jax, jax.numpy as jnp
        import numpy as np
        B, N, D = embeddings.shape
        e = embeddings.reshape(B, N, D // 4, 4)
        ct = jnp.cos(theta)[:, None, None]
        st = jnp.sin(theta)[:, None, None]
        cp = jnp.cos(phi)[:, None, None]
        sp = jnp.sin(phi)[:, None, None]
        x0, x1, x2, x3 = (e[..., 0], e[..., 1], e[..., 2], e[..., 3])
        out = jnp.stack([x0 * ct + x1 * st, -x0 * st + x1 * ct, x2 * cp + x3 * sp, -x2 * sp + x3 * cp], axis=-1)
        return out.reshape(B, N, D)
    x = _L0_cond_ref(x, itok_B_0_7, L0_cond_Wi, L0_cond_bi, L0_cond_Wo, L0_cond_bo, L0_cond_gamma, L0_cond_beta)
    x = _L1_cond_ref(x, condB_theta, condB_phi)
    return x

_drawn_inputs = setup_inputs


def setup_inputs(seed=0):
    import zlib

    import numpy as np

    out = dict(_drawn_inputs(seed))
    spreads = {'L0_cond_bi': (0.0, 0.1),
     'L0_cond_bo': (0.0, 0.1),
     'L0_cond_gamma': (1.0, 0.2),
     'L0_cond_beta': (0.0, 0.1)}
    factors = {}
    for name, (base, spread) in spreads.items():
        noise = np.random.default_rng([zlib.crc32(name.encode()), seed]).standard_normal(out[name].shape)
        drawn = base * np.exp(spread * noise) if base else spread * noise
        out[name] = jnp.asarray(drawn.astype(out[name].dtype))
    for name, factor in factors.items():
        out[name] = (out[name] * factor).astype(out[name].dtype)
    return out
```

```python
from contextlib import ExitStack

import concourse.bass as bass
from concourse import mybir

P = 128
F32 = mybir.dt.float32
F32R = mybir.dt.float32r
I32 = mybir.dt.int32
ALU = mybir.AluOpType
ACT = mybir.ActivationFunctionType

LN_EPS = 1e-12
INV_TWO_PI = 0.15915494309189535
TWO_PI_PARTS = (6.28125, 0.0019350051879882812, 3.0199159819567e-07)
ROUND_TO_INT = 12582912.0
PI_BELOW = 3.1415925
RSQRT_GUESS = 0x5F3759DF
NEWTON_STEPS = 3


class Count:

    def __init__(self, base=0):
        self.base, self.n = base, 0

    def next(self):
        self.n += 1
        return self.base + self.n


def build_ffn_norm_rotate(nc, x, itok, theta, phi, Wi, bi, Wo, bo, gamma, beta, out):
    B, S, H = x.shape
    E, _, I = Wi.shape
    RB = 512
    NT = RB // P
    NK = H // P
    NC = I // P
    NB = B * S // RB
    BB = S // RB
    PAIR = 2
    NP = NC // PAIR
    TRIPLE = 3
    assert (B, BB, NK, NT, NC) == (2, 4, 4, 4, 16)

    x_rows = x.rearrange("b (g p t) h -> (b g) p t h", p=P, t=NT)
    out_rows = out.rearrange("b (g p t) h -> (b g) p t h", p=P, t=NT)
    itok_row = itok.rearrange("(a n) -> a n", a=1)
    theta_row = theta.rearrange("(a n) -> a n", a=1)
    phi_row = phi.rearrange("(a n) -> a n", a=1)

    with ExitStack() as ctx:
        def sb(name, shape, dt=F32):
            return ctx.enter_context(nc.sbuf_tensor(name, shape, dt))

        def sem(name):
            return ctx.enter_context(nc.semaphore(name))

        wi_hi = sb("wi_hi", [P, NK, I], F32R)
        wi_lo = sb("wi_lo", [P, NK, I], F32R)
        wo_hi = sb("wo_hi", [P, NC, H], F32R)
        wo_lo = sb("wo_lo", [P, NC, H], F32R)
        wi_raw = sb("wi_raw", [P, 2, NK, PAIR * P])
        wo_raw = sb("wo_raw", [P, 2, PAIR, H])
        rows = sb("rows", [P, 2, NT, H])
        xT_hi = sb("xT_hi", [P, NK, RB], F32R)
        xT_lo = sb("xT_lo", [P, NK, RB], F32R)
        hT_hi = sb("hT_hi", [P, 2, RB], F32R)
        hT_lo = sb("hT_lo", [P, 2, RB], F32R)
        bo_sb = sb("bo_sb", [P, B, H])
        gain_direct = sb("gain_direct", [P, B, H])
        gain_cross = sb("gain_cross", [P, B, H])
        shift = sb("shift", [P, B, H])
        shift_cross = sb("shift_cross", [P, H])
        cross_part = sb("cross_part", [P, H])
        identity = sb("identity", [P, P])
        bi_rows = sb("bi_rows", [B * NC, P])
        bi_cols = sb("bi_cols", [P, B * NC])
        angle = sb("angle", [P, 2 * B])
        turns = sb("turns", [P, 2 * B])
        turns_part = sb("turns_part", [P, 2 * B])
        sine = sb("sine", [P, 2 * B])
        minus_sine = sb("minus_sine", [P, 2 * B])
        half_sine = sb("half_sine", [P, 2 * B])
        cosine = sb("cosine", [P, 2 * B])
        stats = sb("stats", [P, NT, 6])
        mean_var = sb("mean_var", [P, NT, 2])
        var = sb("var", [P, NT])
        minus_half_var = sb("minus_half_var", [P, NT])
        half_bits = sb("half_bits", [P, NT], I32)
        rstd = sb("rstd", [P, NT])
        newton = sb("newton", [P, NT])

        acc = [ctx.enter_context(nc.psum_tensor(f"acc{t}", [P, H], F32)) for t in range(NT)]
        h_ps = [ctx.enter_context(nc.psum_tensor(f"h_ps{i}", [P, RB], F32)) for i in range(2)]
        tr_ps = [ctx.enter_context(nc.psum_tensor(f"tr_ps{i}", [P, RB], F32)) for i in range(2)]

        wi_in = [sem(f"wi_in{i}") for i in range(2)]
        wo_in = [sem(f"wo_in{i}") for i in range(2)]
        rows_in = [sem(f"rows_in{i}") for i in range(2)]
        bi_in, angle_in = sem("bi_in"), sem("angle_in")
        param_in = [sem(f"param_in{b}") for b in range(B)]
        stored = sem("stored")
        transposed = sem("transposed")
        bi_transposed = sem("bi_transposed")
        s1_done = sem("s1_done")
        s2_done = sem("s2_done")
        acc_done = sem("acc_done")
        xT_hi_ready = sem("xT_hi_ready")
        h_act_ready = sem("h_act_ready")
        w_hi_ready = sem("w_hi_ready")
        sine_ready = sem("sine_ready")
        xT_lo_ready = sem("xT_lo_ready")
        h_lo_ready = sem("h_lo_ready")
        wi_ready = sem("wi_ready")
        wo_ready = sem("wo_ready")
        acc_free = sem("acc_free")
        norm_step = sem("norm_step")
        out_ready = sem("out_ready")
        bi_ready = sem("bi_ready")
        identity_cleared = sem("identity_cleared")
        identity_ready = sem("identity_ready")
        prep_step = sem("prep_step")
        params_ready = sem("params_ready")
        angle_ready = sem("angle_ready")
        rows_bo_ready = sem("rows_bo_ready")

        block = ctx.enter_context(nc.Block())

        def pairs(ap):
            return ap.rearrange("p (q two) -> p q two", two=2)

        def swapped(ap):
            return pairs(ap)[:, :, ::-1]

        @block.sync
        def _(sp):
            def load_rows(g, slot):
                sp.dma_start(rows[:, slot], x_rows[g]).then_inc(rows_in[slot], 16)

            load_rows(0, 0)
            experts = [sp.value_load(itok_row[0:1, b:b + 1], min_val=0, max_val=E - 1) for b in range(B)]
            for b in range(B):
                sp.dma_start(bi_rows[b * NC:(b + 1) * NC, :], bi[bass.ds(experts[b], 1), :]
                             .rearrange("e (c p) -> (e c) p", p=P)).then_inc(bi_in, 16)
            sp.dma_start(angle[:, 0:B], theta_row.to_broadcast([P, B])).then_inc(angle_in, 16)
            sp.dma_start(angle[:, B:2 * B], phi_row.to_broadcast([P, B])).then_inc(angle_in, 16)
            for b in range(B):
                for src, dst in ((bo, bo_sb), (gamma, gain_direct), (beta, shift)):
                    sp.dma_start(dst[:, b], src[bass.ds(experts[b], 1), :].to_broadcast([P, H]))\
                      .then_inc(param_in[b], 16)
            load_rows(1, 1)

            def recycle(g, slot):
                sp.wait_ge(out_ready, NT * (g + 1))
                sp.dma_start(out_rows[bass.ds(g, 1)].rearrange("a p t h -> (a p) t h"),
                             rows[:, slot]).then_inc(stored, 16)
                sp.wait_ge(stored, 16 * (g + 1))
                sp.dma_start(rows[:, slot], x_rows[bass.ds(g + 2, 1)].rearrange("a p t h -> (a p) t h"))\
                  .then_inc(rows_in[slot], 16)

            with sp.Fori(0, NB // 2 - 1, 1) as pair:
                recycle(2 * pair, 0)
                recycle(2 * pair + 1, 1)
            sp.wait_ge(out_ready, NT * (NB - 1))
            sp.dma_start(out_rows[NB - 2], rows[:, 0]).then_inc(stored, 16)
            for t in range(NT):
                sp.wait_ge(out_ready, NT * (NB - 1) + t + 1)
                sp.dma_start(out_rows[NB - 1, :, t], rows[:, 1, t]).then_inc(stored, 16)
            sp.wait_ge(stored, 16 * (NB - 1 + NT))

        @block.tensor
        def _(pe):
            def transpose_rows(g, slot, ks, first=False):
                for k in ks:
                    if k == 0:
                        pe.wait_ge(rows_in[slot], 16 * (g // 2 + 1))
                    if not (first and k < 2):
                        pe.wait_ge(xT_lo_ready, NK * g + k - 1)
                    for t in range(NT):
                        last = nc.tensor.transpose(tr_ps[k % 2][:, t * P:(t + 1) * P],
                                                   rows[:, slot, t, k * P:(k + 1) * P], identity[:, :])
                    last.then_inc(transposed, 1)

            def s1(g, seq, c, first=False):
                pe.wait_ge(wi_ready, NC * seq + c + 1)
                if not (first and c < 2):
                    pe.wait_ge(h_lo_ready, NC * g + c - 1)
                for k in range(NK):
                    if c == 0:
                        pe.wait_ge(xT_lo_ready, NK * g + k + 1)
                    cols = slice(c * P, (c + 1) * P)
                    for n, (w, v) in enumerate(((wi_hi, xT_hi), (wi_hi, xT_lo), (wi_lo, xT_hi))):
                        last = nc.tensor.matmul(h_ps[c % 2][:, :], w[:, k, cols], v[:, k, :],
                                                start=(k == 0 and n == 0), stop=(k == NK - 1 and n == TRIPLE - 1))
                last.then_inc(s1_done, 1)

            def s2(g, seq, c, tiles, first=False):
                if tiles[0] == 0:
                    pe.wait_ge(wo_ready, NC * seq + c + 1)
                    pe.wait_ge(h_lo_ready, NC * g + c + 1)
                for t in tiles:
                    if c == 0 and not first:
                        pe.wait_ge(acc_free, NT * (g - 1) + t + 1)
                    tile = slice(t * P, (t + 1) * P)
                    for n, (v, w) in enumerate(((hT_hi, wo_hi), (hT_hi, wo_lo), (hT_lo, wo_hi))):
                        last = nc.tensor.matmul(acc[t][:, :], v[:, c % 2, tile], w[:, c, :],
                                                start=(c == 0 and n == 0), stop=(c == NC - 1 and n == TRIPLE - 1))
                    if c == NC - 1:
                        last.then_inc(acc_done, 1)
                if c < NC - 1 and tiles[-1] == NT - 1:
                    last.then_inc(s2_done, 1)

            ALL = range(NT)

            def run_block(g, slot, seq, next_seq, first=False, last=False):
                for c in range(NC - 1):
                    s1(g, seq, c + 1, first)
                    if c == NC - 3 and not last:
                        transpose_rows(g + 1, 1 - slot, (0, 1))
                    if c == NC - 2 and not last:
                        s2(g, seq, c, (0, 1), first)
                        transpose_rows(g + 1, 1 - slot, (2, 3))
                        s2(g, seq, c, (2, 3), first)
                    else:
                        s2(g, seq, c, ALL, first)
                if not last:
                    s1(g + 1, next_seq, 0)
                s2(g, seq, NC - 1, ALL, first)

            pe.wait_ge(identity_ready, 1)
            pe.wait_ge(bi_in, 32)
            nc.tensor.transpose(acc[0][:, 0:B * NC], bi_rows[:, :], identity[0:B * NC, 0:B * NC])\
              .then_inc(bi_transposed, 1)
            pe.wait_ge(bi_ready, 1)
            transpose_rows(0, 0, range(NK), first=True)
            s1(0, 0, 0, first=True)
            run_block(0, 0, 0, 0, first=True)
            run_block(1, 1, 0, 0)
            with pe.Fori(1, NB // 2 - 1, 1) as pair:
                run_block(2 * pair, 0, pair // 2, pair // 2)
                run_block(2 * pair + 1, 1, pair // 2, (pair + 1) // 2)
            run_block(NB - 2, 0, B - 1, B - 1)
            run_block(NB - 1, 1, B - 1, B - 1, last=True)

        @block.scalar
        def _(act):
            experts = [act.value_load(itok_row[0:1, b:b + 1], min_val=0, max_val=E - 1) for b in range(B)]

            def load_wi(q):
                if q >= 2:
                    act.wait_ge(wi_ready, PAIR * (q - 1))
                cols = slice(q % NP * PAIR * P, (q % NP + 1) * PAIR * P)
                act.dma_start(wi_raw[:, q % 2], Wi[bass.ds(experts[q // NP], 1), :, cols]
                              .rearrange("e (k p) n -> p (e k) n", p=P)).then_inc(wi_in[q % 2], 16)

            def load_wo(q):
                if q >= 2:
                    act.wait_ge(wo_ready, PAIR * (q - 1))
                lines = slice(q % NP * PAIR * P, (q % NP + 1) * PAIR * P)
                act.dma_start(wo_raw[:, q % 2], Wo[bass.ds(experts[q // NP], 1), lines, :]
                              .rearrange("e (c p) n -> p (e c) n", p=P)).then_inc(wo_in[q % 2], 16)

            def split_wi(b, c):
                q = b * NP + c // PAIR
                act.wait_ge(wi_in[q % 2], 16 * (q // 2 + 1))
                if b:
                    act.wait_ge(s1_done, NC * (BB - 1) + c + 1)
                part = slice(c % PAIR * P, (c % PAIR + 1) * P)
                nc.scalar.copy(wi_hi[:, :, c * P:(c + 1) * P], wi_raw[:, q % 2, :, part]).then_inc(w_hi_ready, 1)

            def split_wo(b, c):
                q = b * NP + c // PAIR
                act.wait_ge(wo_in[q % 2], 16 * (q // 2 + 1))
                if b:
                    wait_s2(BB - 1, c)
                nc.scalar.copy(wo_hi[:, c, :], wo_raw[:, q % 2, c % PAIR, :]).then_inc(w_hi_ready, 1)

            def wait_s2(g, c):
                if c == NC - 1:
                    act.wait_ge(acc_done, NT * (g + 1))
                else:
                    act.wait_ge(s2_done, (NC - 1) * g + c + 1)

            def gelu(g, c, seq, first=False):
                act.wait_ge(s1_done, NC * g + c + 1)
                if c >= 2:
                    wait_s2(g, c - 2)
                elif not first:
                    wait_s2(g - 1, NC + c - 2)
                bias = bi_cols[:, NC * seq + c:NC * seq + c + 1]
                nc.scalar.activation(hT_hi[:, c % 2, :], h_ps[c % 2][:, :], ACT.Gelu, bias=bias)
                nc.scalar.activation(h_ps[c % 2][:, :], h_ps[c % 2][:, :], ACT.Gelu, bias=bias)\
                  .then_inc(h_act_ready, 1)

            def xT_hi_parts(g, ks, first=False):
                for k in ks:
                    act.wait_ge(transposed, NK * g + k + 1)
                    if k == 0 and not first:
                        act.wait_ge(s1_done, NC * g)
                    nc.scalar.copy(xT_hi[:, k, :], tr_ps[k % 2][:, :]).then_inc(xT_hi_ready, 1)

            def run_block(g, seq, first=False, last=False, split=None):
                for c in range(NC):
                    if c == NC - 1 and not last:
                        xT_hi_parts(g + 1, (0, 1))
                    gelu(g, c, seq, first)
                    if split is not None:
                        split(c)
                if not last:
                    xT_hi_parts(g + 1, (2, 3))

            def split_own(c):
                if c + 2 < NC:
                    split_wi(0, c + 2)
                if c + 1 < NC:
                    split_wo(0, c + 1)
                if c % 2 == 1:
                    load_wi(c // 2 + 2)
                if c % 2 == 0 and c:
                    load_wo(c // 2 + 1)

            def split_next(c):
                split_wi(1, c)
                if c >= 2:
                    split_wo(1, c - 2)
                if c % 2 == 0 and c and NP + c // 2 + 1 < 2 * NP:
                    load_wi(NP + c // 2 + 1)
                if c % 2 == 0 and c >= 4 and NP + c // 2 < 2 * NP:
                    load_wo(NP + c // 2)

            load_wi(0)
            load_wo(0)
            load_wi(1)
            load_wo(1)
            act.wait_ge(angle_ready, 1)
            nc.scalar.activation(sine[:, :], angle[:, :], ACT.Sin)
            nc.scalar.activation(half_sine[:, :], angle[:, :], ACT.Sin, scale=0.5).then_inc(sine_ready, 1)
            split_wi(0, 0)
            xT_hi_parts(0, range(NK), first=True)
            split_wi(0, 1)
            split_wo(0, 0)
            act.wait_ge(bi_ready, 1)
            run_block(0, 0, first=True, split=split_own)
            load_wo(NP + 1)
            with act.Fori(1, BB - 1, 1) as g:
                run_block(g, 0)
            run_block(BB - 1, 0, split=split_next)
            split_wo(1, NC - 2)
            split_wo(1, NC - 1)
            with act.Fori(BB, NB - 1, 1) as g:
                run_block(g, 1)
            run_block(NB - 1, 1, last=True)

        @block.vector
        def _(dve):
            splits = Count()

            def split_wi(b, c):
                q = b * NP + c // PAIR
                dve.wait_ge(w_hi_ready, splits.next())
                part = slice(c % PAIR * P, (c % PAIR + 1) * P)
                cols = slice(c * P, (c + 1) * P)
                nc.vector.tensor_tensor(wi_lo[:, :, cols], wi_raw[:, q % 2, :, part],
                                        wi_hi[:, :, cols].bitcast(F32), ALU.subtract).then_inc(wi_ready, 1)

            def split_wo(b, c):
                q = b * NP + c // PAIR
                dve.wait_ge(w_hi_ready, splits.next())
                nc.vector.tensor_tensor(wo_lo[:, c, :], wo_raw[:, q % 2, c % PAIR, :],
                                        wo_hi[:, c, :].bitcast(F32), ALU.subtract).then_inc(wo_ready, 1)

            def hT_lo_part(g, c):
                dve.wait_ge(h_act_ready, NC * g + c + 1)
                nc.vector.tensor_tensor(hT_lo[:, c % 2, :], h_ps[c % 2][:, :], hT_hi[:, c % 2, :].bitcast(F32),
                                        ALU.subtract).then_inc(h_lo_ready, 1)

            def xT_lo_parts(g, ks):
                for k in ks:
                    dve.wait_ge(xT_hi_ready, NK * g + k + 1)
                    nc.vector.tensor_tensor(xT_lo[:, k, :], tr_ps[k % 2][:, :], xT_hi[:, k, :].bitcast(F32),
                                            ALU.subtract).then_inc(xT_lo_ready, 1)

            STEPS = NT + NT + 4 + 3 * NEWTON_STEPS + 3 * NT

            class Norm:

                def __init__(self, g, seq):
                    self.g, self.seq, self.slot = g, seq, g % 2
                    self.step = Count(STEPS * g)

                def tile(self, t):
                    return rows[:, bass.ds(self.slot, 1), t, :].rearrange("p a h -> p (a h)")

                def param(self, table):
                    return table[:, bass.ds(self.seq, 1), :].rearrange("p a h -> p (a h)")

                def link(self, instruction):
                    instruction.then_inc(norm_step, 1)
                    return self.step.next()

                def take_out(self, t):
                    if t == 0:
                        dve.wait_ge(rows_bo_ready, self.g + 1)
                    dve.wait_ge(acc_done, NT * self.g + t + 1)
                    r = self.tile(t)
                    nc.vector.tensor_tensor(r, acc[t][:, :], r, ALU.add).then_inc(acc_free, 1)

                def wait_rows(self):
                    dve.wait_ge(acc_free, NT * self.g + NT)

                def statistics(self):
                    for t in range(NT):
                        self.done = self.link(nc.vector.bn_stats(stats[:, t, :], self.tile(t)))

                def wait_last_step(self):
                    dve.wait_ge(norm_step, self.done)

                def aggregate(self):
                    for t in range(NT):
                        self.done = self.link(nc.vector.bn_aggr(mean_var[:, t, :], stats[:, t, :]))

                def inverse_std(self):
                    dve.wait_ge(norm_step, self.done)
                    done = self.link(nc.vector.tensor_scalar(var[:, :], mean_var[:, :, 1], LN_EPS, None, ALU.add))
                    dve.wait_ge(norm_step, done)
                    self.link(nc.vector.tensor_scalar(minus_half_var[:, :], var[:, :], -0.5, None, ALU.mult))
                    done = self.link(nc.vector.tensor_scalar(half_bits[:, :], var[:, :].bitcast(I32), 1, None,
                                                             ALU.logical_shift_right))
                    dve.wait_ge(norm_step, done)
                    done = self.link(nc.vector.tensor_scalar(rstd[:, :].bitcast(I32), half_bits[:, :], -1.0,
                                                             float(RSQRT_GUESS), ALU.mult, ALU.add))
                    for _ in range(NEWTON_STEPS):
                        dve.wait_ge(norm_step, done)
                        done = self.link(nc.vector.tensor_tensor(newton[:, :], rstd[:, :], rstd[:, :], ALU.mult))
                        dve.wait_ge(norm_step, done)
                        done = self.link(nc.vector.tensor_tensor(newton[:, :], newton[:, :], minus_half_var[:, :],
                                                                 ALU.mult))
                        dve.wait_ge(norm_step, done)
                        done = self.link(nc.vector.scalar_tensor_tensor(out=rstd[:, :], in0=newton[:, :], scalar=1.5,
                                                                        in1=rstd[:, :], op0=ALU.add, op1=ALU.mult))
                    self.done = done

                def affine_and_turn(self, t):
                    r, mean = self.tile(t), mean_var[:, t, 0:1]
                    if t == 0:
                        dve.wait_ge(norm_step, self.done)
                        dve.wait_ge(params_ready, self.seq + 1)
                    self.link(nc.vector.scalar_tensor_tensor(
                        out=cross_part[:, :], in0=r, scalar=mean, in1=self.param(gain_cross),
                        op0=ALU.subtract, op1=ALU.mult))
                    done = self.link(nc.vector.scalar_tensor_tensor(
                        out=r, in0=r, scalar=mean, in1=self.param(gain_direct), op0=ALU.subtract, op1=ALU.mult))
                    dve.wait_ge(norm_step, done)
                    done = self.link(nc.vector.tensor_tensor(pairs(r), pairs(r), swapped(cross_part[:, :]), ALU.add))
                    dve.wait_ge(norm_step, done)
                    nc.vector.scalar_tensor_tensor(
                        out=r, in0=r, scalar=rstd[:, t:t + 1], in1=self.param(shift),
                        op0=ALU.mult, op1=ALU.add).then_inc(out_ready, 1)

            def norm_waits(norm, c):
                if c == 1:
                    norm.wait_rows()
                elif c == 2:
                    norm.wait_last_step()

            def norm_slot(norm, c):
                if c == 0:
                    for t in range(NT):
                        norm.take_out(t)
                elif c == 1:
                    norm.statistics()
                elif c == 2:
                    norm.aggregate()
                    norm.inverse_std()
                elif c - 3 < NT:
                    norm.affine_and_turn(c - 3)

            def run_block(g, last_seq=None, last=False, split=None):
                norm = Norm(g - 1, last_seq) if last_seq is not None else None
                for c in range(NC):
                    if c == NC - 1 and not last:
                        xT_lo_parts(g + 1, (0, 1))
                    if norm is not None:
                        norm_waits(norm, c)
                    hT_lo_part(g, c)
                    if split is not None:
                        split(c)
                    if norm is not None:
                        norm_slot(norm, c)
                if not last:
                    xT_lo_parts(g + 1, (2, 3))

            def split_own(c):
                if c + 2 < NC:
                    split_wi(0, c + 2)
                if c + 1 < NC:
                    split_wo(0, c + 1)

            def split_next(c):
                split_wi(1, c)
                if c >= 2:
                    split_wo(1, c - 2)

            dve.wait_ge(bi_transposed, 1)
            nc.vector.tensor_copy(bi_cols[:, :], acc[0][:, 0:B * NC]).then_inc(bi_ready, 1)
            split_wi(0, 0)
            xT_lo_parts(0, range(NK))
            split_wi(0, 1)
            split_wo(0, 0)
            run_block(0, split=split_own)
            with dve.Fori(1, BB - 1, 1) as g:
                run_block(g, last_seq=0)
            run_block(BB - 1, last_seq=0, split=split_next)
            split_wo(1, NC - 2)
            split_wo(1, NC - 1)
            run_block(BB, last_seq=0)
            with dve.Fori(BB + 1, NB - 1, 1) as g:
                run_block(g, last_seq=1)
            run_block(NB - 1, last_seq=1, last=True)
            norm = Norm(NB - 1, 1)
            for c in range(3 + NT):
                norm_waits(norm, c)
                norm_slot(norm, c)

        @block.gpsimd
        def _(pool):
            nc.gpsimd.memset(identity[:, :], 0.0).then_inc(identity_cleared, 1)
            pool.wait_ge(identity_cleared, 1)
            nc.gpsimd.affine_select(out=identity[:, :], in_=identity[:, :], compare_op=ALU.not_equal, fill=1.0,
                                    base=0, pattern=[[-1, P]], channel_multiplier=1).then_inc(identity_ready, 1)

            step = Count()

            def link(instruction):
                instruction.then_inc(prep_step, 1)
                pool.wait_ge(prep_step, step.next())

            pool.wait_ge(angle_in, 32)
            link(nc.gpsimd.tensor_scalar(turns[:, :], angle[:, :], INV_TWO_PI, ROUND_TO_INT, ALU.mult, ALU.add))
            link(nc.gpsimd.tensor_scalar(turns[:, :], turns[:, :], ROUND_TO_INT, None, ALU.subtract))
            for part in TWO_PI_PARTS:
                link(nc.gpsimd.tensor_scalar(turns_part[:, :], turns[:, :], part, None, ALU.mult))
                link(nc.gpsimd.tensor_tensor(angle[:, :], angle[:, :], turns_part[:, :], ALU.subtract))
            nc.gpsimd.tensor_scalar(angle[:, :], angle[:, :], PI_BELOW, -PI_BELOW, ALU.min, ALU.max)\
              .then_inc(angle_ready, 1)
            pool.wait_ge(sine_ready, 1)
            link(nc.gpsimd.tensor_tensor(cosine[:, :], half_sine[:, :], half_sine[:, :], ALU.mult))
            link(nc.gpsimd.tensor_scalar(cosine[:, :], cosine[:, :], -2.0, 1.0, ALU.mult, ALU.add))
            link(nc.gpsimd.tensor_scalar(minus_sine[:, :], sine[:, :], -1.0, None, ALU.mult))

            def turned(out_ap, in_ap, b, cross):
                o = out_ap.rearrange("p (q f two) -> p q f two", f=2, two=2)
                i = in_ap.rearrange("p (q f two) -> p q f two", f=2, two=2)
                for f in range(2):
                    col = slice(f * B + b, f * B + b + 1)
                    if not cross:
                        link(nc.gpsimd.tensor_scalar(o[:, :, f, :], i[:, :, f, :], cosine[:, col], None, ALU.mult))
                        continue
                    for e, table in ((0, minus_sine), (1, sine)):
                        link(nc.gpsimd.tensor_scalar(o[:, :, f, e], i[:, :, f, e], table[:, col], None, ALU.mult))

            for b in range(B):
                pool.wait_ge(param_in[b], 48)
                turned(gain_cross[:, b], gain_direct[:, b], b, cross=True)
                turned(gain_direct[:, b], gain_direct[:, b], b, cross=False)
                turned(shift_cross[:, :], shift[:, b], b, cross=True)
                turned(shift[:, b], shift[:, b], b, cross=False)
                nc.gpsimd.tensor_tensor(pairs(shift[:, b]), pairs(shift[:, b]), swapped(shift_cross[:, :]), ALU.add)\
                  .then_inc(params_ready, 1)
                pool.wait_ge(params_ready, b + 1)

            with pool.Fori(0, NB, 1) as g:
                pool.wait_ge(transposed, NK * g + NK)
                r = rows[:, bass.ds(g % 2, 1), :, :].rearrange("p a t h -> p (a t) h")
                b = bo_sb[:, bass.ds(g // BB, 1), :].to_broadcast([P, NT, H])
                nc.gpsimd.tensor_tensor(r, r, b, ALU.add).then_inc(rows_bo_ready, 1)


_INS = ["x", "itok_B_0_7", "condB_theta", "condB_phi", "L0_cond_Wi", "L0_cond_bi", "L0_cond_Wo", "L0_cond_bo",
        "L0_cond_gamma", "L0_cond_beta"]


def kernel(**inputs):
    import numpy as _np
    import concourse.bacc as _bacc
    from concourse import mybir as _mybir
    from concourse.bass_utils import run_bass_kernel_spmd as _run

    nc = _bacc.Bacc("TRN2", target_bir_lowering=False, num_devices=1)
    arrays, args = {}, []
    for name in _INS:
        a = _np.ascontiguousarray(inputs[name])
        arrays[f"in_{name}_dram"] = a
        args.append(nc.dram_tensor(f"in_{name}_dram", a.shape, _mybir.dt.from_np(a.dtype), kind="ExternalInput").ap())
    x = arrays["in_x_dram"]
    out = nc.dram_tensor("out_0_dram", x.shape, _mybir.dt.float32, kind="ExternalOutput").ap()
    build_ffn_norm_rotate(nc, *args, out)
    r = _run(nc, [arrays], core_ids=[0])
    return r.results[0]["out_0_dram"]
```

```python
from contextlib import ExitStack

import concourse.bass as bass
from concourse import mybir

P = 128
F32 = mybir.dt.float32
F32R = mybir.dt.float32r
I32 = mybir.dt.int32
ALU = mybir.AluOpType
ACT = mybir.ActivationFunctionType

LN_EPS = 1e-12
INV_TWO_PI = 0.15915494309189535
TWO_PI_PARTS = (6.28125, 0.0019350051879882812, 3.0199159819567e-07)
ROUND_TO_INT = 12582912.0
PI_BELOW = 3.1415925
RSQRT_GUESS = 0x5F3759DF
NEWTON_STEPS = 3


class Count:

    def __init__(self, base=0):
        self.base, self.n = base, 0

    def next(self):
        self.n += 1
        return self.base + self.n


def build_ffn_norm_rotate(nc, x, itok, theta, phi, Wi, bi, Wo, bo, gamma, beta, out):
    B, S, H = x.shape
    E, _, I = Wi.shape
    RB = 512
    NT = RB // P
    NK = H // P
    NC = I // P
    NB = B * S // RB
    BB = S // RB
    PAIR = 2
    NP = NC // PAIR
    TRIPLE = 3
    assert (B, BB, NK, NT, NC) == (2, 4, 4, 4, 16)

    x_rows = x.rearrange("b (g p t) h -> (b g) p t h", p=P, t=NT)
    out_rows = out.rearrange("b (g p t) h -> (b g) p t h", p=P, t=NT)
    itok_row = itok.rearrange("(a n) -> a n", a=1)
    theta_row = theta.rearrange("(a n) -> a n", a=1)
    phi_row = phi.rearrange("(a n) -> a n", a=1)

    with ExitStack() as ctx:
        def sb(name, shape, dt=F32):
            return ctx.enter_context(nc.sbuf_tensor(name, shape, dt))

        def sem(name):
            return ctx.enter_context(nc.semaphore(name))

        wi_hi = sb("wi_hi", [P, NK, I], F32R)
        wi_lo = sb("wi_lo", [P, NK, I], F32R)
        wo_hi = sb("wo_hi", [P, NC, H], F32R)
        wo_lo = sb("wo_lo", [P, NC, H], F32R)
        wi_raw = sb("wi_raw", [P, 2, NK, PAIR * P])
        wo_raw = sb("wo_raw", [P, 2, PAIR, H])
        rows = sb("rows", [P, 2, NT, H])
        xT_hi = sb("xT_hi", [P, NK, RB], F32R)
        xT_lo = sb("xT_lo", [P, NK, RB], F32R)
        hT_hi = sb("hT_hi", [P, 2, RB], F32R)
        hT_lo = sb("hT_lo", [P, 2, RB], F32R)
        bo_sb = sb("bo_sb", [P, B, H])
        gain_direct = sb("gain_direct", [P, B, H])
        gain_cross = sb("gain_cross", [P, B, H])
        shift = sb("shift", [P, B, H])
        shift_cross = sb("shift_cross", [P, H])
        cross_part = sb("cross_part", [P, H])
        identity = sb("identity", [P, P])
        bi_rows = sb("bi_rows", [B * NC, P])
        bi_cols = sb("bi_cols", [P, B * NC])
        angle = sb("angle", [P, 2 * B])
        turns = sb("turns", [P, 2 * B])
        turns_part = sb("turns_part", [P, 2 * B])
        sine = sb("sine", [P, 2 * B])
        minus_sine = sb("minus_sine", [P, 2 * B])
        half_sine = sb("half_sine", [P, 2 * B])
        cosine = sb("cosine", [P, 2 * B])
        stats = sb("stats", [P, NT, 6])
        mean_var = sb("mean_var", [P, NT, 2])
        var = sb("var", [P, NT])
        minus_half_var = sb("minus_half_var", [P, NT])
        half_bits = sb("half_bits", [P, NT], I32)
        rstd = sb("rstd", [P, NT])
        newton = sb("newton", [P, NT])
        gelu_warm = sb("gelu_warm", [P, 1])

        acc = [ctx.enter_context(nc.psum_tensor(f"acc{t}", [P, H], F32)) for t in range(NT)]
        h_ps = [ctx.enter_context(nc.psum_tensor(f"h_ps{i}", [P, RB], F32)) for i in range(2)]
        tr_ps = [ctx.enter_context(nc.psum_tensor(f"tr_ps{i}", [P, RB], F32)) for i in range(2)]

        wi_in = [sem(f"wi_in{i}") for i in range(2)]
        wo_in = [sem(f"wo_in{i}") for i in range(2)]
        rows_in = [sem(f"rows_in{i}") for i in range(2)]
        first_rows_in = [sem(f"first_rows_in{t}") for t in range(NT)]
        first_wi_in = sem("first_wi_in")
        bi_in, angle_in = sem("bi_in"), sem("angle_in")
        param_in = [sem(f"param_in{b}") for b in range(B)]
        stored = sem("stored")
        transposed = sem("transposed")
        bi_transposed = sem("bi_transposed")
        s1_done = sem("s1_done")
        s2_done = sem("s2_done")
        acc_done = sem("acc_done")
        xT_hi_ready = sem("xT_hi_ready")
        h_act_ready = sem("h_act_ready")
        w_hi_ready = sem("w_hi_ready")
        sine_ready = sem("sine_ready")
        xT_lo_ready = sem("xT_lo_ready")
        h_lo_ready = sem("h_lo_ready")
        wi_ready = sem("wi_ready")
        wo_ready = sem("wo_ready")
        acc_free = sem("acc_free")
        norm_step = sem("norm_step")
        out_ready = sem("out_ready")
        bi_ready = sem("bi_ready")
        identity_cleared = sem("identity_cleared")
        identity_ready = sem("identity_ready")
        prep_step = sem("prep_step")
        params_ready = sem("params_ready")
        angle_ready = sem("angle_ready")
        rows_bo_ready = sem("rows_bo_ready")

        block = ctx.enter_context(nc.Block())

        def tiles_of(ap):
            return ap.rearrange("p (t r) -> p t r", t=NT)

        def pairs(ap):
            return ap.rearrange("p (q two) -> p q two", two=2)

        def swapped(ap):
            return pairs(ap)[:, :, ::-1]

        @block.sync
        def _(sp):
            for t in range(NT):
                sp.dma_start(rows[:, 0, t], x_rows[0, :, t]).then_inc(first_rows_in[t], 16)
            experts = [sp.value_load(itok_row[0:1, b:b + 1], min_val=0, max_val=E - 1) for b in range(B)]
            first_wi = Wi[bass.ds(experts[0], 1)].rearrange("e (k p) n -> p (e k) n", p=P)
            first_wo = Wo[bass.ds(experts[0], 1)].rearrange("e (c p) n -> p (e c) n", p=P)
            sp.dma_start(wi_raw[:, 0, :, 0:P], first_wi[:, :, 0:P]).then_inc(first_wi_in, 16)
            for b in range(B):
                sp.dma_start(bi_rows[b * NC:(b + 1) * NC, :], bi[bass.ds(experts[b], 1), :]
                             .rearrange("e (c p) -> (e c) p", p=P)).then_inc(bi_in, 16)
            sp.dma_start(wi_raw[:, 0, :, P:PAIR * P], first_wi[:, :, P:PAIR * P]).then_inc(wi_in[0], 16)
            sp.dma_start(wo_raw[:, 0], first_wo[:, 0:PAIR]).then_inc(wo_in[0], 16)
            sp.dma_start(wi_raw[:, 1], first_wi[:, :, PAIR * P:2 * PAIR * P]).then_inc(wi_in[1], 16)
            sp.dma_start(wo_raw[:, 1], first_wo[:, PAIR:2 * PAIR]).then_inc(wo_in[1], 16)
            sp.dma_start(angle[:, 0:B], theta_row.to_broadcast([P, B])).then_inc(angle_in, 16)
            sp.dma_start(angle[:, B:2 * B], phi_row.to_broadcast([P, B])).then_inc(angle_in, 16)
            for b in range(B):
                for src, dst in ((bo, bo_sb), (gamma, gain_direct), (beta, shift)):
                    sp.dma_start(dst[:, b], src[bass.ds(experts[b], 1), :].to_broadcast([P, H]))\
                      .then_inc(param_in[b], 16)
            sp.dma_start(rows[:, 1], x_rows[1]).then_inc(rows_in[1], 16)

            def recycle(g, slot):
                sp.wait_ge(out_ready, NT * (g + 1))
                sp.dma_start(out_rows[bass.ds(g, 1)].rearrange("a p t h -> (a p) t h"),
                             rows[:, slot]).then_inc(stored, 16)
                sp.wait_ge(stored, 16 * (g + 1))
                sp.dma_start(rows[:, slot], x_rows[bass.ds(g + 2, 1)].rearrange("a p t h -> (a p) t h"))\
                  .then_inc(rows_in[slot], 16)

            with sp.Fori(0, NB // 2 - 1, 1) as pair:
                recycle(2 * pair, 0)
                recycle(2 * pair + 1, 1)
            sp.wait_ge(out_ready, NT * (NB - 1))
            sp.dma_start(out_rows[NB - 2], rows[:, 0]).then_inc(stored, 16)
            for t in range(NT):
                sp.wait_ge(out_ready, NT * (NB - 1) + t + 1)
                sp.dma_start(out_rows[NB - 1, :, t], rows[:, 1, t]).then_inc(stored, 16)
            sp.wait_ge(stored, 16 * (NB - 1 + NT))

        @block.tensor
        def _(pe):
            def transpose_first_rows():
                for t in range(NT):
                    pe.wait_ge(first_rows_in[t], 16)
                    for k in range(NK):
                        one = nc.tensor.transpose(acc[k][:, t * P:(t + 1) * P],
                                                  rows[:, 0, t, k * P:(k + 1) * P], identity[:, :])
                        if t == NT - 1:
                            one.then_inc(transposed, 1)

            def transpose_rows(g, slot, ks):
                for k in ks:
                    if k == 0:
                        pe.wait_ge(rows_in[slot], 16 * (g // 2 + slot))
                    pe.wait_ge(xT_lo_ready, NK * g + k - 1)
                    for t in range(NT):
                        last = nc.tensor.transpose(tr_ps[k % 2][:, t * P:(t + 1) * P],
                                                   rows[:, slot, t, k * P:(k + 1) * P], identity[:, :])
                    last.then_inc(transposed, 1)

            def s1(g, seq, c, first=False):
                pe.wait_ge(wi_ready, NC * seq + c + 1)
                if not (first and c < 2):
                    pe.wait_ge(h_lo_ready, NC * g + c - 1)
                for k in range(NK):
                    if c == 0:
                        pe.wait_ge(xT_lo_ready, NK * g + k + 1)
                    cols = slice(c * P, (c + 1) * P)
                    for n, (w, v) in enumerate(((wi_hi, xT_hi), (wi_hi, xT_lo), (wi_lo, xT_hi))):
                        last = nc.tensor.matmul(h_ps[c % 2][:, :], w[:, k, cols], v[:, k, :],
                                                start=(k == 0 and n == 0), stop=(k == NK - 1 and n == TRIPLE - 1))
                last.then_inc(s1_done, 1)

            def s2(g, seq, c, tiles, first=False):
                if tiles[0] == 0:
                    pe.wait_ge(wo_ready, NC * seq + c + 1)
                    pe.wait_ge(h_lo_ready, NC * g + c + 1)
                for t in tiles:
                    if c == 0 and not first:
                        pe.wait_ge(acc_free, NT * (g - 1) + t + 1)
                    tile = slice(t * P, (t + 1) * P)
                    for n, (v, w) in enumerate(((hT_hi, wo_hi), (hT_hi, wo_lo), (hT_lo, wo_hi))):
                        last = nc.tensor.matmul(acc[t][:, :], v[:, c % 2, tile], w[:, c, :],
                                                start=(c == 0 and n == 0), stop=(c == NC - 1 and n == TRIPLE - 1))
                    if c == NC - 1:
                        last.then_inc(acc_done, 1)
                if c < NC - 1 and tiles[-1] == NT - 1:
                    last.then_inc(s2_done, 1)

            def s2_tile_of_last_block(t):
                pe.wait_ge(acc_free, NT * (NB - 2) + t + 1)
                for c in range(NC):
                    if t == 0:
                        pe.wait_ge(h_lo_ready, NC * (NB - 1) + c + 1)
                    cols = slice(c * P, (c + 1) * P)
                    for n, (v, w) in enumerate(((wi_hi, wo_hi), (wi_hi, wo_lo), (wi_lo, wo_hi))):
                        last = nc.tensor.matmul(acc[t][:, :], v[:, t, cols], w[:, c, :],
                                                start=(c == 0 and n == 0), stop=(c == NC - 1 and n == TRIPLE - 1))
                last.then_inc(acc_done, 1)

            ALL = range(NT)

            def run_block(g, slot, seq, next_seq, first=False):
                for c in range(NC - 1):
                    s1(g, seq, c + 1, first)
                    if c == NC - 3:
                        transpose_rows(g + 1, 1 - slot, (0, 1))
                    if c == NC - 2:
                        s2(g, seq, c, (0, 1), first)
                        transpose_rows(g + 1, 1 - slot, (2, 3))
                        s2(g, seq, c, (2, 3), first)
                    else:
                        s2(g, seq, c, ALL, first)
                s1(g + 1, next_seq, 0)
                s2(g, seq, NC - 1, ALL, first)

            pe.wait_ge(identity_ready, 1)
            transpose_first_rows()
            pe.wait_ge(bi_in, 32)
            nc.tensor.transpose(tr_ps[0][:, 0:B * NC], bi_rows[:, :], identity[0:B * NC, 0:B * NC])\
              .then_inc(bi_transposed, 1)
            s1(0, 0, 0, first=True)
            run_block(0, 0, 0, 0, first=True)
            run_block(1, 1, 0, 0)
            with pe.Fori(1, NB // 2 - 1, 1) as pair:
                run_block(2 * pair, 0, pair // 2, pair // 2)
                run_block(2 * pair + 1, 1, pair // 2, (pair + 1) // 2)
            run_block(NB - 2, 0, B - 1, B - 1)
            for c in range(1, NC):
                s1(NB - 1, B - 1, c)
            for t in ALL:
                s2_tile_of_last_block(t)

        @block.scalar
        def _(act):
            experts = [act.value_load(itok_row[0:1, b:b + 1], min_val=0, max_val=E - 1) for b in range(B)]

            def load_wi(q):
                act.wait_ge(wi_ready, PAIR * (q - 1))
                cols = slice(q % NP * PAIR * P, (q % NP + 1) * PAIR * P)
                act.dma_start(wi_raw[:, q % 2], Wi[bass.ds(experts[q // NP], 1), :, cols]
                              .rearrange("e (k p) n -> p (e k) n", p=P)).then_inc(wi_in[q % 2], 16)

            def load_wo(q):
                act.wait_ge(wo_ready, PAIR * (q - 1))
                lines = slice(q % NP * PAIR * P, (q % NP + 1) * PAIR * P)
                act.dma_start(wo_raw[:, q % 2], Wo[bass.ds(experts[q // NP], 1), lines, :]
                              .rearrange("e (c p) n -> p (e c) n", p=P)).then_inc(wo_in[q % 2], 16)

            def split_wi(b, c):
                q = b * NP + c // PAIR
                if b == 0 and c == 0:
                    act.wait_ge(first_wi_in, 16)
                else:
                    act.wait_ge(wi_in[q % 2], 16 * (q // 2 + 1))
                if b:
                    act.wait_ge(s1_done, NC * (BB - 1) + c + 1)
                part = slice(c % PAIR * P, (c % PAIR + 1) * P)
                nc.scalar.copy(wi_hi[:, :, c * P:(c + 1) * P], wi_raw[:, q % 2, :, part]).then_inc(w_hi_ready, 1)

            def split_wo(b, c):
                q = b * NP + c // PAIR
                act.wait_ge(wo_in[q % 2], 16 * (q // 2 + 1))
                if b:
                    wait_s2(BB - 1, c)
                nc.scalar.copy(wo_hi[:, c, :], wo_raw[:, q % 2, c % PAIR, :]).then_inc(w_hi_ready, 1)

            def wait_s2(g, c):
                if c == NC - 1:
                    act.wait_ge(acc_done, NT * (g + 1))
                else:
                    act.wait_ge(s2_done, (NC - 1) * g + c + 1)

            def gelu(g, c, seq, first=False):
                act.wait_ge(s1_done, NC * g + c + 1)
                if c >= 2:
                    wait_s2(g, c - 2)
                elif not first:
                    wait_s2(g - 1, NC + c - 2)
                bias = bi_cols[:, NC * seq + c:NC * seq + c + 1]
                nc.scalar.activation(hT_hi[:, c % 2, :], h_ps[c % 2][:, :], ACT.Gelu, bias=bias)
                nc.scalar.activation(h_ps[c % 2][:, :], h_ps[c % 2][:, :], ACT.Gelu, bias=bias)\
                  .then_inc(h_act_ready, 1)

            def gelu_of_last_block(c):
                act.wait_ge(s1_done, NC * (NB - 1) + c + 1)
                bias = bi_cols[:, NC * (B - 1) + c:NC * (B - 1) + c + 1]
                nc.scalar.activation(wi_hi[:, :, c * P:(c + 1) * P], tiles_of(h_ps[c % 2][:, :]), ACT.Gelu, bias=bias)
                nc.scalar.activation(h_ps[c % 2][:, :], h_ps[c % 2][:, :], ACT.Gelu, bias=bias)\
                  .then_inc(h_act_ready, 1)

            def xT_hi_parts_of_first_block(ks):
                for k in ks:
                    act.wait_ge(transposed, k + 1)
                    nc.scalar.copy(xT_hi[:, k, :], acc[k][:, :]).then_inc(xT_hi_ready, 1)

            def xT_hi_parts(g, ks):
                for k in ks:
                    act.wait_ge(transposed, NK * g + k + 1)
                    if k == 0:
                        act.wait_ge(s1_done, NC * g)
                    nc.scalar.copy(xT_hi[:, k, :], tr_ps[k % 2][:, :]).then_inc(xT_hi_ready, 1)

            def run_block(g, seq, first=False, split=None):
                for c in range(NC):
                    if c == NC - 1:
                        xT_hi_parts(g + 1, (0, 1))
                    gelu(g, c, seq, first)
                    if split is not None:
                        split(c)
                xT_hi_parts(g + 1, (2, 3))

            def split_own(c):
                if c == NC // 2:
                    act.wait_ge(angle_ready, 1)
                    nc.scalar.activation(sine[:, :], angle[:, :], ACT.Sin)
                    nc.scalar.activation(half_sine[:, :], angle[:, :], ACT.Sin, scale=0.5).then_inc(sine_ready, 1)
                if c + 2 < NC:
                    split_wi(0, c + 2)
                if c + 1 < NC:
                    split_wo(0, c + 1)
                if c % 2 == 1:
                    load_wi(c // 2 + 2)
                if c % 2 == 0 and c:
                    load_wo(c // 2 + 1)

            def split_next(c):
                split_wi(1, c)
                if c >= 2:
                    split_wo(1, c - 2)
                if c % 2 == 0 and c and NP + c // 2 + 1 < 2 * NP:
                    load_wi(NP + c // 2 + 1)
                if c % 2 == 0 and c >= 4 and NP + c // 2 < 2 * NP:
                    load_wo(NP + c // 2)

            act.wait_ge(identity_ready, 1)
            nc.scalar.activation(gelu_warm[:, :], identity[:, 0:1], ACT.Gelu)
            xT_hi_parts_of_first_block((0, 1))
            split_wi(0, 0)
            xT_hi_parts_of_first_block((2, 3))
            split_wi(0, 1)
            split_wo(0, 0)
            act.wait_ge(bi_ready, 1)
            run_block(0, 0, first=True, split=split_own)
            load_wo(NP + 1)
            with act.Fori(1, BB - 1, 1) as g:
                run_block(g, 0)
            run_block(BB - 1, 0, split=split_next)
            split_wo(1, NC - 2)
            split_wo(1, NC - 1)
            with act.Fori(BB, NB - 1, 1) as g:
                run_block(g, 1)
            for c in range(NC):
                gelu_of_last_block(c)

        @block.vector
        def _(dve):
            splits = Count()

            def split_wi(b, c):
                q = b * NP + c // PAIR
                dve.wait_ge(w_hi_ready, splits.next())
                part = slice(c % PAIR * P, (c % PAIR + 1) * P)
                cols = slice(c * P, (c + 1) * P)
                nc.vector.tensor_tensor(wi_lo[:, :, cols], wi_raw[:, q % 2, :, part],
                                        wi_hi[:, :, cols].bitcast(F32), ALU.subtract).then_inc(wi_ready, 1)

            def split_wo(b, c):
                q = b * NP + c // PAIR
                dve.wait_ge(w_hi_ready, splits.next())
                nc.vector.tensor_tensor(wo_lo[:, c, :], wo_raw[:, q % 2, c % PAIR, :],
                                        wo_hi[:, c, :].bitcast(F32), ALU.subtract).then_inc(wo_ready, 1)

            def hT_lo_part(g, c):
                dve.wait_ge(h_act_ready, NC * g + c + 1)
                nc.vector.tensor_tensor(hT_lo[:, c % 2, :], h_ps[c % 2][:, :], hT_hi[:, c % 2, :].bitcast(F32),
                                        ALU.subtract).then_inc(h_lo_ready, 1)

            def hT_lo_part_of_last_block(c):
                dve.wait_ge(h_act_ready, NC * (NB - 1) + c + 1)
                cols = slice(c * P, (c + 1) * P)
                nc.vector.tensor_tensor(wi_lo[:, :, cols], tiles_of(h_ps[c % 2][:, :]), wi_hi[:, :, cols].bitcast(F32),
                                        ALU.subtract).then_inc(h_lo_ready, 1)

            def xT_lo_parts_of_first_block(ks):
                for k in ks:
                    dve.wait_ge(xT_hi_ready, k + 1)
                    nc.vector.tensor_tensor(xT_lo[:, k, :], acc[k][:, :], xT_hi[:, k, :].bitcast(F32),
                                            ALU.subtract).then_inc(xT_lo_ready, 1)

            def xT_lo_parts(g, ks):
                for k in ks:
                    dve.wait_ge(xT_hi_ready, NK * g + k + 1)
                    nc.vector.tensor_tensor(xT_lo[:, k, :], tr_ps[k % 2][:, :], xT_hi[:, k, :].bitcast(F32),
                                            ALU.subtract).then_inc(xT_lo_ready, 1)

            STEPS = NT + NT + 4 + 3 * NEWTON_STEPS + 3 * NT

            class Norm:

                def __init__(self, g, seq):
                    self.g, self.seq, self.slot = g, seq, g % 2
                    self.step = Count(STEPS * g)

                def tile(self, t):
                    return rows[:, bass.ds(self.slot, 1), t, :].rearrange("p a h -> p (a h)")

                def param(self, table):
                    return table[:, bass.ds(self.seq, 1), :].rearrange("p a h -> p (a h)")

                def link(self, instruction):
                    instruction.then_inc(norm_step, 1)
                    return self.step.next()

                def take_out(self, t):
                    if t == 0:
                        dve.wait_ge(rows_bo_ready, self.g + 1)
                    dve.wait_ge(acc_done, NT * self.g + t + 1)
                    r = self.tile(t)
                    nc.vector.tensor_tensor(r, acc[t][:, :], r, ALU.add).then_inc(acc_free, 1)

                def wait_rows(self, upto=NT):
                    dve.wait_ge(acc_free, NT * self.g + upto)

                def statistics(self, tiles):
                    for t in tiles:
                        self.done = self.link(nc.vector.bn_stats(stats[:, t, :], self.tile(t)))

                def wait_last_step(self):
                    dve.wait_ge(norm_step, self.done)

                def aggregate(self, tiles):
                    for t in tiles:
                        self.done = self.link(nc.vector.bn_aggr(mean_var[:, t, :], stats[:, t, :]))

                def guess(self, tiles):
                    cols = slice(tiles[0], tiles[-1] + 1)
                    self.wait_last_step()
                    self.link(nc.vector.tensor_scalar(minus_half_var[:, cols], mean_var[:, cols, 1], -0.5,
                                                      -0.5 * LN_EPS, ALU.mult, ALU.add))
                    self.done = self.link(nc.vector.tensor_scalar(var[:, cols], mean_var[:, cols, 1], LN_EPS, None,
                                                                  ALU.add))
                    self.wait_last_step()
                    self.done = self.link(nc.vector.tensor_scalar(half_bits[:, cols], var[:, cols].bitcast(I32), 1,
                                                                  None, ALU.logical_shift_right))
                    self.wait_last_step()
                    self.done = self.link(nc.vector.tensor_scalar(rstd[:, cols].bitcast(I32), half_bits[:, cols], -1.0,
                                                                  float(RSQRT_GUESS), ALU.mult, ALU.add))

                def newton_steps(self, tiles):
                    cols = slice(tiles[0], tiles[-1] + 1)
                    y, part = rstd[:, cols], newton[:, cols]
                    for _ in range(NEWTON_STEPS):
                        self.wait_last_step()
                        self.done = self.link(nc.vector.tensor_tensor(part, y, y, ALU.mult))
                        self.wait_last_step()
                        self.done = self.link(nc.vector.tensor_tensor(part, part, minus_half_var[:, cols], ALU.mult))
                        self.wait_last_step()
                        self.done = self.link(nc.vector.scalar_tensor_tensor(out=y, in0=part, scalar=1.5, in1=y,
                                                                             op0=ALU.add, op1=ALU.mult))

                def affine_and_turn(self, t):
                    r, mean = self.tile(t), mean_var[:, t, 0:1]
                    if t == 0:
                        dve.wait_ge(params_ready, self.seq + 1)
                    self.wait_last_step()
                    self.link(nc.vector.scalar_tensor_tensor(
                        out=cross_part[:, :], in0=r, scalar=mean, in1=self.param(gain_cross),
                        op0=ALU.subtract, op1=ALU.mult))
                    self.done = self.link(nc.vector.scalar_tensor_tensor(
                        out=r, in0=r, scalar=mean, in1=self.param(gain_direct), op0=ALU.subtract, op1=ALU.mult))
                    self.wait_last_step()
                    self.done = self.link(nc.vector.tensor_tensor(pairs(r), pairs(r), swapped(cross_part[:, :]),
                                                                  ALU.add))
                    self.wait_last_step()
                    nc.vector.scalar_tensor_tensor(
                        out=r, in0=r, scalar=rstd[:, t:t + 1], in1=self.param(shift),
                        op0=ALU.mult, op1=ALU.add).then_inc(out_ready, 1)

            ALL = range(NT)

            def norm_waits(norm, c):
                if c == 1:
                    norm.wait_rows()
                elif c == 2:
                    norm.wait_last_step()

            def norm_slot(norm, c):
                if c == 0:
                    for t in ALL:
                        norm.take_out(t)
                elif c == 1:
                    norm.statistics(ALL)
                elif c == 2:
                    norm.aggregate(ALL)
                    norm.guess(ALL)
                    norm.newton_steps(ALL)
                elif c - 3 < NT:
                    norm.affine_and_turn(c - 3)

            def run_last_block():
                norm = Norm(NB - 2, B - 1)
                for c in range(NC):
                    hT_lo_part_of_last_block(c)
                    if c in (0, 1):
                        norm.take_out(2 * c)
                        norm.take_out(2 * c + 1)
                    elif c in (2, 3):
                        norm.wait_rows(2 * (c - 2) + 2)
                        norm.statistics((2 * (c - 2), 2 * (c - 2) + 1))
                    elif c == 4:
                        norm.wait_last_step()
                        norm.aggregate(ALL)
                        norm.guess(ALL)
                    elif c == 5:
                        norm.newton_steps(ALL)
                    elif c % 2 == 0 and c < 6 + 2 * NT:
                        norm.affine_and_turn(c // 2 - 3)

            def norm_last_tile(norm, t):
                norm.take_out(t)
                norm.wait_rows(t + 1)
                norm.statistics((t,))
                norm.wait_last_step()
                norm.aggregate((t,))
                norm.guess((t,))
                norm.newton_steps((t,))
                norm.affine_and_turn(t)

            def run_block(g, last_seq=None, split=None):
                norm = Norm(g - 1, last_seq) if last_seq is not None else None
                for c in range(NC):
                    if c == NC - 1:
                        xT_lo_parts(g + 1, (0, 1))
                    if norm is not None:
                        norm_waits(norm, c)
                    hT_lo_part(g, c)
                    if split is not None:
                        split(c)
                    if norm is not None:
                        norm_slot(norm, c)
                xT_lo_parts(g + 1, (2, 3))

            def split_own(c):
                if c + 2 < NC:
                    split_wi(0, c + 2)
                if c + 1 < NC:
                    split_wo(0, c + 1)

            def split_next(c):
                split_wi(1, c)
                if c >= 2:
                    split_wo(1, c - 2)

            xT_lo_parts_of_first_block((0, 1))
            split_wi(0, 0)
            xT_lo_parts_of_first_block((2, 3))
            dve.wait_ge(bi_transposed, 1)
            nc.vector.tensor_copy(bi_cols[:, :], tr_ps[0][:, 0:B * NC]).then_inc(bi_ready, 1)
            split_wi(0, 1)
            split_wo(0, 0)
            run_block(0, split=split_own)
            with dve.Fori(1, BB - 1, 1) as g:
                run_block(g, last_seq=0)
            run_block(BB - 1, last_seq=0, split=split_next)
            split_wo(1, NC - 2)
            split_wo(1, NC - 1)
            run_block(BB, last_seq=0)
            with dve.Fori(BB + 1, NB - 1, 1) as g:
                run_block(g, last_seq=1)
            run_last_block()
            last_norm = Norm(NB - 1, B - 1)
            for t in ALL:
                norm_last_tile(last_norm, t)

        @block.gpsimd
        def _(pool):
            nc.gpsimd.memset(identity[:, :], 0.0).then_inc(identity_cleared, 1)
            pool.wait_ge(identity_cleared, 1)
            nc.gpsimd.affine_select(out=identity[:, :], in_=identity[:, :], compare_op=ALU.not_equal, fill=1.0,
                                    base=0, pattern=[[-1, P]], channel_multiplier=1).then_inc(identity_ready, 1)

            step = Count()

            def link(instruction):
                instruction.then_inc(prep_step, 1)
                pool.wait_ge(prep_step, step.next())

            pool.wait_ge(angle_in, 32)
            link(nc.gpsimd.tensor_scalar(turns[:, :], angle[:, :], INV_TWO_PI, ROUND_TO_INT, ALU.mult, ALU.add))
            link(nc.gpsimd.tensor_scalar(turns[:, :], turns[:, :], ROUND_TO_INT, None, ALU.subtract))
            for part in TWO_PI_PARTS:
                link(nc.gpsimd.tensor_scalar(turns_part[:, :], turns[:, :], part, None, ALU.mult))
                link(nc.gpsimd.tensor_tensor(angle[:, :], angle[:, :], turns_part[:, :], ALU.subtract))
            nc.gpsimd.tensor_scalar(angle[:, :], angle[:, :], PI_BELOW, -PI_BELOW, ALU.min, ALU.max)\
              .then_inc(angle_ready, 1)
            pool.wait_ge(sine_ready, 1)
            link(nc.gpsimd.tensor_tensor(cosine[:, :], half_sine[:, :], half_sine[:, :], ALU.mult))
            link(nc.gpsimd.tensor_scalar(cosine[:, :], cosine[:, :], -2.0, 1.0, ALU.mult, ALU.add))
            link(nc.gpsimd.tensor_scalar(minus_sine[:, :], sine[:, :], -1.0, None, ALU.mult))

            def turned(out_ap, in_ap, b, cross):
                o = out_ap.rearrange("p (q f two) -> p q f two", f=2, two=2)
                i = in_ap.rearrange("p (q f two) -> p q f two", f=2, two=2)
                for f in range(2):
                    col = slice(f * B + b, f * B + b + 1)
                    if not cross:
                        link(nc.gpsimd.tensor_scalar(o[:, :, f, :], i[:, :, f, :], cosine[:, col], None, ALU.mult))
                        continue
                    for e, table in ((0, minus_sine), (1, sine)):
                        link(nc.gpsimd.tensor_scalar(o[:, :, f, e], i[:, :, f, e], table[:, col], None, ALU.mult))

            for b in range(B):
                pool.wait_ge(param_in[b], 48)
                turned(gain_cross[:, b], gain_direct[:, b], b, cross=True)
                turned(gain_direct[:, b], gain_direct[:, b], b, cross=False)
                turned(shift_cross[:, :], shift[:, b], b, cross=True)
                turned(shift[:, b], shift[:, b], b, cross=False)
                nc.gpsimd.tensor_tensor(pairs(shift[:, b]), pairs(shift[:, b]), swapped(shift_cross[:, :]), ALU.add)\
                  .then_inc(params_ready, 1)
                pool.wait_ge(params_ready, b + 1)

            with pool.Fori(0, NB, 1) as g:
                pool.wait_ge(transposed, NK * g + NK)
                r = rows[:, bass.ds(g % 2, 1), :, :].rearrange("p a t h -> p (a t) h")
                b = bo_sb[:, bass.ds(g // BB, 1), :].to_broadcast([P, NT, H])
                nc.gpsimd.tensor_tensor(r, r, b, ALU.add).then_inc(rows_bo_ready, 1)


_INS = ["x", "itok_B_0_7", "condB_theta", "condB_phi", "L0_cond_Wi", "L0_cond_bi", "L0_cond_Wo", "L0_cond_bo",
        "L0_cond_gamma", "L0_cond_beta"]


def kernel(**inputs):
    import numpy as _np
    import concourse.bacc as _bacc
    from concourse import mybir as _mybir
    from concourse.bass_utils import run_bass_kernel_spmd as _run

    nc = _bacc.Bacc("TRN2", target_bir_lowering=False, num_devices=1)
    arrays, args = {}, []
    for name in _INS:
        a = _np.ascontiguousarray(inputs[name])
        arrays[f"in_{name}_dram"] = a
        args.append(nc.dram_tensor(f"in_{name}_dram", a.shape, _mybir.dt.from_np(a.dtype), kind="ExternalInput").ap())
    x = arrays["in_x_dram"]
    out = nc.dram_tensor("out_0_dram", x.shape, _mybir.dt.float32, kind="ExternalOutput").ap()
    build_ffn_norm_rotate(nc, *args, out)
    r = _run(nc, [arrays], core_ids=[0])
    return r.results[0]["out_0_dram"]
```

```python
from contextlib import ExitStack

import concourse.bass as bass
from concourse import mybir

P = 128
F32 = mybir.dt.float32
F32R = mybir.dt.float32r
I32 = mybir.dt.int32
ALU = mybir.AluOpType
ACT = mybir.ActivationFunctionType

LN_EPS = 1e-12
INV_TWO_PI = 0.15915494309189535
TWO_PI_PARTS = (6.28125, 0.0019350051879882812, 3.0199159819567e-07)
ROUND_TO_INT = 12582912.0
PI_BELOW = 3.1415925
RSQRT_GUESS = 0x5F3759DF - 2 ** 22 - 2 ** 30
NEWTON_STEPS = 3


class Count:

    def __init__(self, base=0):
        self.base, self.n = base, 0

    def next(self):
        self.n += 1
        return self.base + self.n


def build_ffn_norm_rotate(nc, x, itok, theta, phi, Wi, bi, Wo, bo, gamma, beta, out):
    B, S, H = x.shape
    E, _, I = Wi.shape
    RB = 512
    NT = RB // P
    NK = H // P
    NC = I // P
    NB = B * S // RB
    BB = S // RB
    Q = 32
    NG = P // Q
    TRIPLE = 3
    WARM_UPS = 14
    HALVES = (slice(0, H // 2), slice(H // 2, H))
    assert (B, BB, NK, NT, NC) == (2, 4, 4, 4, 16)

    x_rows = x.rearrange("b (g t p) h -> (b g) p t h", p=P, t=NT)
    out_rows = out.rearrange("b (g t p) h -> (b g) p t h", p=P, t=NT)
    x_squares = x.rearrange("b (g m i) (G f) -> (b g) G i m f", i=Q, m=RB // Q, G=NG)
    itok_row = itok.rearrange("(a n) -> a n", a=1)
    theta_row = theta.rearrange("(a n) -> a n", a=1)
    phi_row = phi.rearrange("(a n) -> a n", a=1)

    with ExitStack() as ctx:
        def sb(name, shape, dt=F32):
            return ctx.enter_context(nc.sbuf_tensor(name, shape, dt))

        def sem(name):
            return ctx.enter_context(nc.semaphore(name))

        wi_hi = sb("wi_hi", [P, NK, I], F32R)
        wi_lo = sb("wi_lo", [P, NK, I], F32R)
        wo_hi = sb("wo_hi", [P, NC, H], F32R)
        wo_lo = sb("wo_lo", [P, NC, H], F32R)
        wi_raw = sb("wi_raw", [P, 2, NK, P])
        wo_raw = sb("wo_raw", [P, 2, H])
        rows = sb("rows", [P, 2, NT, H])
        x_sq = sb("x_sq", [P, RB // Q, P])
        xT_hi = sb("xT_hi", [P, NK, RB], F32R)
        xT_lo = sb("xT_lo", [P, NK, RB], F32R)
        hT_hi = sb("hT_hi", [P, 2, RB], F32R)
        hT_lo = sb("hT_lo", [P, 2, RB], F32R)
        bo_sb = sb("bo_sb", [P, B, H])
        gain_direct = sb("gain_direct", [P, B, H])
        gain_cross = sb("gain_cross", [P, B, H])
        shift = sb("shift", [P, B, H])
        shift_cross = sb("shift_cross", [P, H])
        cross_part = sb("cross_part", [P, H])
        identity = sb("identity", [P, P])
        bi_rows = sb("bi_rows", [B * NC, P])
        bi_cols = sb("bi_cols", [P, B * NC])
        angle = sb("angle", [P, 2 * B])
        turns = sb("turns", [P, 2 * B])
        turns_part = sb("turns_part", [P, 2 * B])
        sine = sb("sine", [P, 2 * B])
        minus_sine = sb("minus_sine", [P, 2 * B])
        half_sine = sb("half_sine", [P, 2 * B])
        cosine = sb("cosine", [P, 2 * B])
        stats = sb("stats", [P, NT + 1, 6])
        mean_var = sb("mean_var", [P, NT, 2])
        minus_half_var = sb("minus_half_var", [P, NT])
        rstd = sb("rstd", [P, NT])
        newton = sb("newton", [P, NT])
        gelu_warm = sb("gelu_warm", [P, 1])

        acc = [ctx.enter_context(nc.psum_tensor(f"acc{t}", [P, H], F32)) for t in range(NT)]
        h_ps = [ctx.enter_context(nc.psum_tensor(f"h_ps{i}", [P, RB], F32)) for i in range(2)]
        tr_ps = [ctx.enter_context(nc.psum_tensor(f"tr_ps{i}", [P, RB], F32)) for i in range(2)]

        xT_banks = [tr_ps[k % 2] for k in range(NK)]
        xT_banks_of_first = [tr_ps[0], tr_ps[1], acc[2], acc[3]]

        half_banks = [tr_ps[0], acc[NT - 1]]

        wi_in = [sem(f"wi_in{i}") for i in range(2)]
        wo_in = [sem(f"wo_in{i}") for i in range(2)]
        rows_in = sem("rows_in")
        squares_in = sem("squares_in")
        bi_in, angle_in = sem("bi_in"), sem("angle_in")
        param_in = [sem(f"param_in{b}") for b in range(B)]
        stored = sem("stored")
        bi_transposed = sem("bi_transposed")
        s1_done = sem("s1_done")
        xT_used = sem("xT_used")
        s2_done = sem("s2_done")
        acc_done = sem("acc_done")
        xT_hi_ready = sem("xT_hi_ready")
        h_act_ready = sem("h_act_ready")
        w_hi_ready = sem("w_hi_ready")
        sine_ready = sem("sine_ready")
        transposed = sem("transposed")
        xT_lo_ready = sem("xT_lo_ready")
        h_lo_ready = sem("h_lo_ready")
        wi_ready = sem("wi_ready")
        wo_ready = sem("wo_ready")
        acc_free = sem("acc_free")
        norm_step = sem("norm_step")
        out_ready = sem("out_ready")
        bi_ready = sem("bi_ready")
        identity_cleared = sem("identity_cleared")
        identity_ready = sem("identity_ready")
        prep_step = sem("prep_step")
        params_ready = sem("params_ready")
        angle_ready = sem("angle_ready")
        rows_bo_ready = sem("rows_bo_ready")

        block = ctx.enter_context(nc.Block())

        def tiles_of(ap):
            return ap.rearrange("p (t r) -> p t r", t=NT)

        def pairs(ap):
            return ap.rearrange("p (q two) -> p q two", two=2)

        def swapped(ap):
            return pairs(ap)[:, :, ::-1]

        def load_wi(eng, expert, q):
            if q >= 2:
                eng.wait_ge(wi_ready, q - 1)
            cols = slice(q % NC * P, (q % NC + 1) * P)
            for G in range(NG):
                eng.dma_start(wi_raw[G * Q:(G + 1) * Q, q % 2], Wi[bass.ds(expert, 1), G * P:(G + 1) * P, cols]
                              .rearrange("e (k j) n -> j (e k) n", j=Q)).then_inc(wi_in[q % 2], 16)

        @block.sync
        def _(sp):
            def load_wo(q):
                if q >= 2:
                    sp.wait_ge(wo_ready, q - 1)
                sp.dma_start(wo_raw[:, q % 2], Wo[bass.ds(experts[q // NC], 1), q % NC * P:(q % NC + 1) * P, :]
                             .rearrange("e p n -> (e p) n")).then_inc(wo_in[q % 2], 16)

            def load_squares(g):
                if g > 0:
                    sp.wait_ge(transposed, NK * g)
                for G in range(NG):
                    sp.dma_start(x_sq[G * Q:(G + 1) * Q], x_squares[g, G]).then_inc(squares_in, 16)

            def load_rows(g):
                if g > 0:
                    sp.wait_ge(rows_in, 16 * g)
                sp.dma_start(rows[:, g % 2], x_rows[g]).then_inc(rows_in, 16)

            def store(g):
                sp.wait_ge(out_ready, NT * (g + 1))
                sp.dma_start(out_rows[g], rows[:, g % 2]).then_inc(stored, 16)

            def reload(g):
                sp.wait_ge(stored, 16 * (g + 1))
                load_rows(g + 2)

            load_squares(0)
            experts = [sp.value_load(itok_row[0:1, 0:1], min_val=0, max_val=E - 1)]
            load_wi(sp, experts[0], 1)
            load_wo(0)
            experts.append(sp.value_load(itok_row[0:1, 1:2], min_val=0, max_val=E - 1))
            for b in range(B):
                sp.dma_start(bi_rows[b * NC:(b + 1) * NC, :], bi[bass.ds(experts[b], 1), :]
                             .rearrange("e (c p) -> (e c) p", p=P)).then_inc(bi_in, 16)
            load_wo(1)
            for q in range(2, NC + 2):
                load_wi(sp, experts[q // NC], q)
                load_wo(q)
                if q == 3:
                    sp.dma_start(angle[:, 0:B], theta_row.to_broadcast([P, B])).then_inc(angle_in, 16)
                    sp.dma_start(angle[:, B:2 * B], phi_row.to_broadcast([P, B])).then_inc(angle_in, 16)
                    load_rows(0)
                if q == 5:
                    load_squares(1)
                if q in (6, 8):
                    b = q // 2 - 3
                    for src, dst in ((bo, bo_sb), (gamma, gain_direct), (beta, shift)):
                        sp.dma_start(dst[:, b], src[bass.ds(experts[b], 1), :].to_broadcast([P, H]))\
                          .then_inc(param_in[b], 16)
            load_rows(1)

            def run_block(g):
                load_squares(g + 1)
                store(g - 1)
                reload(g - 1)

            for g in range(1, BB - 1):
                run_block(g)
            load_squares(BB)
            for c in range(1, NC):
                if c + 1 < NC:
                    load_wi(sp, experts[1], NC + c + 1)
                if c >= 3:
                    load_wo(NC + c - 1)
                if c == 8:
                    store(BB - 2)
                if c == 10:
                    reload(BB - 2)
            load_wo(2 * NC - 1)
            for g in range(BB, NB - 1):
                run_block(g)
            store(NB - 2)
            last_pieces = [(t, slice(0, H)) for t in range(NT - 1)] + [(NT - 1, cols) for cols in HALVES]
            for i, (t, cols) in enumerate(last_pieces):
                sp.wait_ge(out_ready, NT * (NB - 1) + i + 1)
                sp.dma_start(out_rows[NB - 1, :, t, cols], rows[:, (NB - 1) % 2, t, cols]).then_inc(stored, 16)
            sp.wait_ge(stored, 16 * (NB - 1 + len(last_pieces)))

        @block.tensor
        def _(pe):
            def s1(g, seq, c, first=False):
                pe.wait_ge(wi_ready, NC * seq + c + 1)
                if not (first and c < 2):
                    pe.wait_ge(h_lo_ready, NC * g + c - 1)
                for k in range(NK):
                    if c == 0:
                        pe.wait_ge(xT_lo_ready, NK * g + k + 1)
                    cols = slice(c * P, (c + 1) * P)
                    for n, (w, v) in enumerate(((wi_hi, xT_hi), (wi_hi, xT_lo), (wi_lo, xT_hi))):
                        last = nc.tensor.matmul(h_ps[c % 2][:, :], w[:, k, cols], v[:, k, :],
                                                start=(k == 0 and n == 0), stop=(k == NK - 1 and n == TRIPLE - 1))
                    if c == NC - 1 and k < NK - 1:
                        last.then_inc(xT_used, 1)
                last.then_inc(s1_done, 1)

            def s2(g, seq, c, first=False):
                pe.wait_ge(wo_ready, NC * seq + c + 1)
                pe.wait_ge(h_lo_ready, NC * g + c + 1)
                for t in range(NT):
                    if c == 0 and not first:
                        pe.wait_ge(acc_free, NT * (g - 1) + t + 1)
                    tile = slice(t * P, (t + 1) * P)
                    for n, (v, w) in enumerate(((hT_hi, wo_hi), (hT_hi, wo_lo), (hT_lo, wo_hi))):
                        last = nc.tensor.matmul(acc[t][:, :], v[:, c % 2, tile], w[:, c, :],
                                                start=(c == 0 and n == 0), stop=(c == NC - 1 and n == TRIPLE - 1))
                    if c == NC - 1:
                        last.then_inc(acc_done, 1)
                if c < NC - 1:
                    last.then_inc(s2_done, 1)

            def s2_tile_of_last_block(t, bank, out_cols):
                pe.wait_ge(acc_free, NT * (NB - 2) + t + 1)
                for c in range(NC):
                    if t == 0:
                        pe.wait_ge(h_lo_ready, NC * (NB - 1) + c + 1)
                    cols = slice(c * P, (c + 1) * P)
                    for n, (v, w) in enumerate(((wi_hi, wo_hi), (wi_hi, wo_lo), (wi_lo, wo_hi))):
                        last = nc.tensor.matmul(bank[:, out_cols], v[:, t, cols], w[:, c, out_cols],
                                                start=(c == 0 and n == 0), stop=(c == NC - 1 and n == TRIPLE - 1))
                last.then_inc(acc_done, 1)

            def run_block(g, seq, next_seq, first=False):
                for c in range(NC - 1):
                    s1(g, seq, c + 1, first)
                    s2(g, seq, c, first)
                s1(g + 1, next_seq, 0)
                s2(g, seq, NC - 1, first)

            def first_s1():
                pe.wait_ge(w_hi_ready, 1)
                for n, (w, v) in enumerate(((wi_hi, xT_hi), (wi_lo, xT_hi), (wi_hi, xT_lo))):
                    if n == 1:
                        pe.wait_ge(wi_ready, 1)
                    for k in range(NK):
                        if n == 0:
                            pe.wait_ge(xT_hi_ready, k + 1)
                        elif n == 2:
                            pe.wait_ge(xT_lo_ready, k + 1)
                        last = nc.tensor.matmul(h_ps[0][:, :], w[:, k, 0:P], v[:, k, :], start=(n == 0 and k == 0),
                                                stop=(n == TRIPLE - 1 and k == NK - 1))
                last.then_inc(s1_done, 1)

            pe.wait_ge(identity_ready, 1)
            for _ in range(WARM_UPS):
                nc.tensor.matmul(acc[1][:, 0:P], identity[:, :], identity[:, :], start=True, stop=True)
            first_s1()
            pe.wait_ge(bi_in, 32)
            nc.tensor.transpose(acc[0][:, 0:B * NC], bi_rows[:, :], identity[0:B * NC, 0:B * NC])\
              .then_inc(bi_transposed, 1)
            run_block(0, 0, 0, first=True)
            with pe.Fori(1, NB - 1, 1) as g:
                run_block(g, g // BB, (g + 1) // BB)
            for c in range(1, NC):
                s1(NB - 1, B - 1, c)
            for t in range(NT - 1):
                s2_tile_of_last_block(t, acc[t], slice(0, H))
            for bank, out_cols in zip(half_banks, HALVES):
                s2_tile_of_last_block(NT - 1, bank, out_cols)

        @block.scalar
        def _(act):
            def split_wi(b, c):
                q = b * NC + c
                act.wait_ge(wi_in[q % 2], 16 * NG * (q // 2 + 1))
                if b:
                    act.wait_ge(s1_done, NC * (BB - 1) + c + 1)
                nc.scalar.copy(wi_hi[:, :, c * P:(c + 1) * P], wi_raw[:, q % 2]).then_inc(w_hi_ready, 1)

            def split_wo(b, c):
                q = b * NC + c
                act.wait_ge(wo_in[q % 2], 16 * (q // 2 + 1))
                if b:
                    wait_s2(BB - 1, c)
                nc.scalar.copy(wo_hi[:, c, :], wo_raw[:, q % 2]).then_inc(w_hi_ready, 1)

            def wait_s2(g, c):
                if c == NC - 1:
                    act.wait_ge(acc_done, NT * (g + 1))
                else:
                    act.wait_ge(s2_done, (NC - 1) * g + c + 1)

            def gelu(g, c, seq, first=False):
                act.wait_ge(s1_done, NC * g + c + 1)
                if c >= 2:
                    wait_s2(g, c - 2)
                elif not first:
                    wait_s2(g - 1, NC + c - 2)
                bias = bi_cols[:, NC * seq + c:NC * seq + c + 1]
                nc.scalar.activation(hT_hi[:, c % 2, :], h_ps[c % 2][:, :], ACT.Gelu, bias=bias)
                nc.scalar.activation(h_ps[c % 2][:, :], h_ps[c % 2][:, :], ACT.Gelu, bias=bias)\
                  .then_inc(h_act_ready, 1)

            def gelu_of_last_block(c):
                act.wait_ge(s1_done, NC * (NB - 1) + c + 1)
                bias = bi_cols[:, NC * (B - 1) + c:NC * (B - 1) + c + 1]
                nc.scalar.activation(wi_hi[:, :, c * P:(c + 1) * P], tiles_of(h_ps[c % 2][:, :]), ACT.Gelu, bias=bias)
                nc.scalar.activation(h_ps[c % 2][:, :], h_ps[c % 2][:, :], ACT.Gelu, bias=bias)\
                  .then_inc(h_act_ready, 1)

            def xT_hi_parts(g, ks, banks=xT_banks, first=False):
                for k in ks:
                    act.wait_ge(transposed, NK * g + k + 1)
                    if k == NK - 1 and not first:
                        act.wait_ge(s1_done, NC * g)
                    elif not first:
                        act.wait_ge(xT_used, (NK - 1) * (g - 1) + k + 1)
                    nc.scalar.copy(xT_hi[:, k, :], banks[k][:, :]).then_inc(xT_hi_ready, 1)

            def run_block(g, seq, first=False, split=None):
                for c in range(NC):
                    if c == NC - 1:
                        xT_hi_parts(g + 1, (0, 1, 2))
                    gelu(g, c, seq, first)
                    if split is not None:
                        split(c)
                xT_hi_parts(g + 1, (3,))

            def split_own(c):
                if c == NC // 2:
                    act.wait_ge(angle_ready, 1)
                    nc.scalar.activation(sine[:, :], angle[:, :], ACT.Sin)
                    nc.scalar.activation(half_sine[:, :], angle[:, :], ACT.Sin, scale=0.5).then_inc(sine_ready, 1)
                if c + 2 < NC:
                    split_wi(0, c + 2)
                if c + 1 < NC:
                    split_wo(0, c + 1)

            def split_next(c):
                split_wi(1, c)
                if c >= 2:
                    split_wo(1, c - 2)

            def split_rest(c):
                if c in (1, 2):
                    split_wo(1, NC - 3 + c)

            load_wi(act, act.value_load(itok_row[0:1, 0:1], min_val=0, max_val=E - 1), 0)
            act.wait_ge(identity_ready, 1)
            nc.scalar.activation(gelu_warm[:, :], identity[:, 0:1], ACT.Gelu)
            split_wi(0, 0)
            xT_hi_parts(0, range(NK), xT_banks_of_first, first=True)
            split_wi(0, 1)
            split_wo(0, 0)
            act.wait_ge(bi_ready, 1)
            run_block(0, 0, first=True, split=split_own)
            with act.Fori(1, BB - 1, 1) as g:
                run_block(g, 0)
            run_block(BB - 1, 0, split=split_next)
            run_block(BB, 1, split=split_rest)
            with act.Fori(BB + 1, NB - 1, 1) as g:
                run_block(g, 1)
            for c in range(NC):
                gelu_of_last_block(c)

        @block.vector
        def _(dve):
            splits = Count(1)

            def split_wi(b, c):
                dve.wait_ge(w_hi_ready, splits.next())
                cols = slice(c * P, (c + 1) * P)
                nc.vector.tensor_tensor(wi_lo[:, :, cols], wi_raw[:, (b * NC + c) % 2],
                                        wi_hi[:, :, cols].bitcast(F32), ALU.subtract).then_inc(wi_ready, 1)

            def split_wo(b, c):
                dve.wait_ge(w_hi_ready, splits.next())
                nc.vector.tensor_tensor(wo_lo[:, c, :], wo_raw[:, (b * NC + c) % 2],
                                        wo_hi[:, c, :].bitcast(F32), ALU.subtract).then_inc(wo_ready, 1)

            def hT_lo_part(g, c):
                dve.wait_ge(h_act_ready, NC * g + c + 1)
                nc.vector.tensor_tensor(hT_lo[:, c % 2, :], h_ps[c % 2][:, :], hT_hi[:, c % 2, :].bitcast(F32),
                                        ALU.subtract).then_inc(h_lo_ready, 1)

            def hT_lo_part_of_last_block(c):
                dve.wait_ge(h_act_ready, NC * (NB - 1) + c + 1)
                cols = slice(c * P, (c + 1) * P)
                nc.vector.tensor_tensor(wi_lo[:, :, cols], tiles_of(h_ps[c % 2][:, :]), wi_hi[:, :, cols].bitcast(F32),
                                        ALU.subtract).then_inc(h_lo_ready, 1)

            def transpose_squares(g, k, banks=xT_banks, first=False):
                if not first:
                    dve.wait_ge(xT_lo_ready, NK * g + k - 1)
                if k == 0:
                    dve.wait_ge(squares_in, 16 * NG * (g + 1))
                nc.vector.transpose(banks[k][:, :].rearrange("p (m j) -> p m j", j=Q),
                                    x_sq[:, :, k * Q:(k + 1) * Q]).then_inc(transposed, 1)

            def xT_lo_parts(g, ks, banks=xT_banks):
                for k in ks:
                    dve.wait_ge(xT_hi_ready, NK * g + k + 1)
                    nc.vector.tensor_tensor(xT_lo[:, k, :], banks[k][:, :], xT_hi[:, k, :].bitcast(F32),
                                            ALU.subtract).then_inc(xT_lo_ready, 1)

            STEPS = NT + NT + 2 + 3 * NEWTON_STEPS + 3 * NT

            class Norm:

                def __init__(self, g, seq):
                    self.g, self.seq, self.slot = g, seq, g % 2
                    self.step = Count(STEPS * g)

                def tile(self, t):
                    return rows[:, bass.ds(self.slot, 1), t, :].rearrange("p a h -> p (a h)")

                def param(self, table):
                    return table[:, bass.ds(self.seq, 1), :].rearrange("p a h -> p (a h)")

                def link(self, instruction):
                    instruction.then_inc(norm_step, 1)
                    return self.step.next()

                def take_out(self, t):
                    if t == 0:
                        dve.wait_ge(rows_bo_ready, self.g + 1)
                    dve.wait_ge(acc_done, NT * self.g + t + 1)
                    r = self.tile(t)
                    nc.vector.tensor_tensor(r, acc[t][:, :], r, ALU.add).then_inc(acc_free, 1)

                def wait_rows(self, upto=NT):
                    dve.wait_ge(acc_free, NT * self.g + upto)

                def statistics(self, tiles):
                    for t in tiles:
                        self.done = self.link(nc.vector.bn_stats(stats[:, t, :], self.tile(t)))

                def wait_last_step(self):
                    dve.wait_ge(norm_step, self.done)

                def aggregate(self, tiles):
                    for t in tiles:
                        self.done = self.link(nc.vector.bn_aggr(mean_var[:, t, :], stats[:, t, :]))

                def guess(self, tiles):
                    cols = slice(tiles[0], tiles[-1] + 1)
                    self.wait_last_step()
                    self.done = self.link(nc.vector.tensor_scalar(minus_half_var[:, cols], mean_var[:, cols, 1], -0.5,
                                                                  -0.5 * LN_EPS, ALU.mult, ALU.add))
                    self.wait_last_step()
                    self.done = self.link(nc.vector.tensor_scalar(
                        rstd[:, cols].bitcast(I32), minus_half_var[:, cols].bitcast(I32), -0.5, float(RSQRT_GUESS),
                        ALU.mult, ALU.add))

                def newton_steps(self, tiles):
                    cols = slice(tiles[0], tiles[-1] + 1)
                    y, part = rstd[:, cols], newton[:, cols]
                    for _ in range(NEWTON_STEPS):
                        self.wait_last_step()
                        self.done = self.link(nc.vector.tensor_tensor(part, y, y, ALU.mult))
                        self.wait_last_step()
                        self.done = self.link(nc.vector.tensor_tensor(part, part, minus_half_var[:, cols], ALU.mult))
                        self.wait_last_step()
                        self.done = self.link(nc.vector.scalar_tensor_tensor(out=y, in0=part, scalar=1.5, in1=y,
                                                                             op0=ALU.add, op1=ALU.mult))

                def affine_and_turn(self, t):
                    self.gains(t)
                    self.turn_and_shift(t)

                def gains(self, t):
                    r, mean = self.tile(t), mean_var[:, t, 0:1]
                    if t == 0:
                        dve.wait_ge(params_ready, self.seq + 1)
                    self.wait_last_step()
                    self.link(nc.vector.scalar_tensor_tensor(
                        out=cross_part[:, :], in0=r, scalar=mean, in1=self.param(gain_cross),
                        op0=ALU.subtract, op1=ALU.mult))
                    self.done = self.link(nc.vector.scalar_tensor_tensor(
                        out=r, in0=r, scalar=mean, in1=self.param(gain_direct), op0=ALU.subtract, op1=ALU.mult))

                def turn_and_shift(self, t):
                    r = self.tile(t)
                    self.wait_last_step()
                    self.done = self.link(nc.vector.tensor_tensor(pairs(r), pairs(r), swapped(cross_part[:, :]),
                                                                  ALU.add))
                    self.wait_last_step()
                    nc.vector.scalar_tensor_tensor(
                        out=r, in0=r, scalar=rstd[:, t:t + 1], in1=self.param(shift),
                        op0=ALU.mult, op1=ALU.add).then_inc(out_ready, 1)

            ALL = range(NT)

            def norm_waits(norm, c):
                if c == 1:
                    norm.wait_rows()
                elif c == 2:
                    norm.wait_last_step()

            def norm_slot(norm, c):
                if c == 0:
                    for t in ALL:
                        norm.take_out(t)
                elif c == 1:
                    norm.statistics(ALL)
                elif c == 2:
                    norm.aggregate(ALL)
                    norm.guess(ALL)
                    norm.newton_steps(ALL)
                elif c - 3 < NT:
                    norm.affine_and_turn(c - 3)

            def run_last_block():
                norm = Norm(NB - 2, B - 1)
                for c in range(NC):
                    hT_lo_part_of_last_block(c)
                    if c in (0, 1):
                        norm.take_out(2 * c)
                        norm.take_out(2 * c + 1)
                    elif c in (2, 3):
                        norm.wait_rows(2 * (c - 2) + 2)
                        norm.statistics((2 * (c - 2), 2 * (c - 2) + 1))
                    elif c == 4:
                        norm.wait_last_step()
                        norm.aggregate(ALL)
                        norm.guess(ALL)
                    elif c == 5:
                        norm.newton_steps(ALL)
                    elif c % 2 == 0 and c < 6 + 2 * NT:
                        norm.gains(c // 2 - 3)
                    elif c < 6 + 2 * NT:
                        norm.turn_and_shift((c - 1) // 2 - 3)

            def newton_product(norm, t):
                y = rstd[:, t:t + 1]
                norm.done = norm.link(nc.vector.scalar_tensor_tensor(
                    out=newton[:, t:t + 1], in0=y, scalar=minus_half_var[:, t:t + 1], in1=y, op0=ALU.mult,
                    op1=ALU.mult))

            def newton_step_end(norm, t):
                norm.wait_last_step()
                y = rstd[:, t:t + 1]
                norm.done = norm.link(nc.vector.scalar_tensor_tensor(
                    out=y, in0=newton[:, t:t + 1], scalar=1.5, in1=y, op0=ALU.add, op1=ALU.mult))

            def norm_last_tile(norm, t):
                norm.take_out(t)
                norm.wait_rows(t + 1)
                norm.statistics((t,))
                norm.wait_last_step()
                norm.aggregate((t,))
                norm.guess((t,))
                for _ in range(NEWTON_STEPS):
                    norm.wait_last_step()
                    newton_product(norm, t)
                    newton_step_end(norm, t)
                norm.affine_and_turn(t)

            def norm_very_last_tile(norm):
                t, seq = NT - 1, B - 1
                r, mean, rs, half_v = norm.tile(t), mean_var[:, t, 0:1], rstd[:, t:t + 1], minus_half_var[:, t:t + 1]
                for i, (bank, cols) in enumerate(zip(half_banks, HALVES)):
                    dve.wait_ge(acc_done, NT * NB + i)
                    nc.vector.tensor_tensor(r[:, cols], bank[:, cols], r[:, cols], ALU.add).then_inc(acc_free, 1)
                    dve.wait_ge(acc_free, NT * NB + i)
                    done = norm.link(nc.vector.bn_stats(stats[:, t + i, :], r[:, cols]))
                dve.wait_ge(norm_step, done)
                done = norm.link(nc.vector.bn_aggr(mean_var[:, t, :], stats[:, t:t + 2, :]))
                dve.wait_ge(norm_step, done)
                chain = norm.link(nc.vector.tensor_scalar(half_v, mean_var[:, t, 1:2], -0.5, -0.5 * LN_EPS, ALU.mult,
                                                          ALU.add))
                norm.link(nc.vector.scalar_tensor_tensor(
                    out=cross_part[:, :], in0=r, scalar=mean, in1=gain_cross[:, seq], op0=ALU.subtract, op1=ALU.mult))
                dve.wait_ge(norm_step, chain)
                chain = norm.link(nc.vector.tensor_scalar(rs.bitcast(I32), half_v.bitcast(I32), -0.5,
                                                          float(RSQRT_GUESS), ALU.mult, ALU.add))
                parts = norm.link(nc.vector.scalar_tensor_tensor(
                    out=r, in0=r, scalar=mean, in1=gain_direct[:, seq], op0=ALU.subtract, op1=ALU.mult))
                dve.wait_ge(norm_step, chain)
                newton_product(norm, t)
                dve.wait_ge(norm_step, parts)
                norm.link(nc.vector.tensor_tensor(pairs(r), pairs(r), swapped(cross_part[:, :]), ALU.add))
                newton_step_end(norm, t)
                for _ in range(NEWTON_STEPS - 1):
                    norm.wait_last_step()
                    newton_product(norm, t)
                    newton_step_end(norm, t)
                norm.wait_last_step()
                for cols in HALVES:
                    nc.vector.scalar_tensor_tensor(out=r[:, cols], in0=r[:, cols], scalar=rs,
                                                   in1=shift[:, seq, cols], op0=ALU.mult, op1=ALU.add)\
                      .then_inc(out_ready, 1)

            def run_block(g, last_seq=None, split=None):
                norm = Norm(g - 1, last_seq) if last_seq is not None else None
                for c in range(NC):
                    if c == NC - 1:
                        xT_lo_parts(g + 1, (0,))
                        transpose_squares(g + 1, 2)
                        xT_lo_parts(g + 1, (1,))
                        transpose_squares(g + 1, 3)
                        xT_lo_parts(g + 1, (2,))
                    if norm is not None:
                        norm_waits(norm, c)
                    hT_lo_part(g, c)
                    if split is not None:
                        split(c)
                    if norm is not None:
                        norm_slot(norm, c)
                    if c == NC - 3:
                        transpose_squares(g + 1, 0)
                        transpose_squares(g + 1, 1)
                xT_lo_parts(g + 1, (3,))

            def split_own(c):
                if c + 2 < NC:
                    split_wi(0, c + 2)
                if c + 1 < NC:
                    split_wo(0, c + 1)

            def split_next(c):
                split_wi(1, c)
                if c >= 2:
                    split_wo(1, c - 2)

            def split_rest(c):
                if c in (1, 2):
                    split_wo(1, NC - 3 + c)

            for k in range(NK):
                transpose_squares(0, k, xT_banks_of_first, first=True)
            xT_lo_parts(0, range(NK), xT_banks_of_first)
            dve.wait_ge(wi_ready, 1)
            split_wi(0, 1)
            dve.wait_ge(bi_transposed, 1)
            nc.vector.tensor_copy(bi_cols[:, :], acc[0][:, 0:B * NC]).then_inc(bi_ready, 1)
            split_wo(0, 0)
            run_block(0, split=split_own)
            with dve.Fori(1, BB - 1, 1) as g:
                run_block(g, last_seq=0)
            run_block(BB - 1, last_seq=0, split=split_next)
            run_block(BB, last_seq=0, split=split_rest)
            with dve.Fori(BB + 1, NB - 1, 1) as g:
                run_block(g, last_seq=1)
            run_last_block()
            last_norm = Norm(NB - 1, B - 1)
            for t in range(NT - 1):
                norm_last_tile(last_norm, t)
            norm_very_last_tile(last_norm)

        @block.gpsimd
        def _(pool):
            nc.gpsimd.memset(identity[:, :], 0.0).then_inc(identity_cleared, 1)
            pool.wait_ge(identity_cleared, 1)
            nc.gpsimd.affine_select(out=identity[:, :], in_=identity[:, :], compare_op=ALU.not_equal, fill=1.0,
                                    base=0, pattern=[[-1, P]], channel_multiplier=1).then_inc(identity_ready, 1)

            pool.wait_ge(w_hi_ready, 1)
            nc.gpsimd.tensor_tensor(wi_lo[:, :, 0:P], wi_raw[:, 0], wi_hi[:, :, 0:P].bitcast(F32), ALU.subtract)\
              .then_inc(wi_ready, 1)

            step = Count()

            def link(instruction):
                instruction.then_inc(prep_step, 1)
                pool.wait_ge(prep_step, step.next())

            pool.wait_ge(angle_in, 32)
            link(nc.gpsimd.tensor_scalar(turns[:, :], angle[:, :], INV_TWO_PI, ROUND_TO_INT, ALU.mult, ALU.add))
            link(nc.gpsimd.tensor_scalar(turns[:, :], turns[:, :], ROUND_TO_INT, None, ALU.subtract))
            for part in TWO_PI_PARTS:
                link(nc.gpsimd.tensor_scalar(turns_part[:, :], turns[:, :], part, None, ALU.mult))
                link(nc.gpsimd.tensor_tensor(angle[:, :], angle[:, :], turns_part[:, :], ALU.subtract))
            nc.gpsimd.tensor_scalar(angle[:, :], angle[:, :], PI_BELOW, -PI_BELOW, ALU.min, ALU.max)\
              .then_inc(angle_ready, 1)
            pool.wait_ge(sine_ready, 1)
            link(nc.gpsimd.tensor_tensor(cosine[:, :], half_sine[:, :], half_sine[:, :], ALU.mult))
            link(nc.gpsimd.tensor_scalar(cosine[:, :], cosine[:, :], -2.0, 1.0, ALU.mult, ALU.add))
            link(nc.gpsimd.tensor_scalar(minus_sine[:, :], sine[:, :], -1.0, None, ALU.mult))

            def turned(out_ap, in_ap, b, cross):
                o = out_ap.rearrange("p (q f two) -> p q f two", f=2, two=2)
                i = in_ap.rearrange("p (q f two) -> p q f two", f=2, two=2)
                for f in range(2):
                    col = slice(f * B + b, f * B + b + 1)
                    if not cross:
                        link(nc.gpsimd.tensor_scalar(o[:, :, f, :], i[:, :, f, :], cosine[:, col], None, ALU.mult))
                        continue
                    for e, table in ((0, minus_sine), (1, sine)):
                        link(nc.gpsimd.tensor_scalar(o[:, :, f, e], i[:, :, f, e], table[:, col], None, ALU.mult))

            for b in range(B):
                pool.wait_ge(param_in[b], 48)
                turned(gain_cross[:, b], gain_direct[:, b], b, cross=True)
                turned(gain_direct[:, b], gain_direct[:, b], b, cross=False)
                turned(shift_cross[:, :], shift[:, b], b, cross=True)
                turned(shift[:, b], shift[:, b], b, cross=False)
                nc.gpsimd.tensor_tensor(pairs(shift[:, b]), pairs(shift[:, b]), swapped(shift_cross[:, :]), ALU.add)\
                  .then_inc(params_ready, 1)
                pool.wait_ge(params_ready, b + 1)

            with pool.Fori(0, NB, 1) as g:
                pool.wait_ge(rows_in, 16 * (g + 1))
                r = rows[:, bass.ds(g % 2, 1), :, :].rearrange("p a t h -> p (a t) h")
                nc.gpsimd.tensor_tensor(r, r, bo_sb[:, bass.ds(g // BB, 1), :].to_broadcast([P, NT, H]), ALU.add)\
                  .then_inc(rows_bo_ready, 1)


_INS = ["x", "itok_B_0_7", "condB_theta", "condB_phi", "L0_cond_Wi", "L0_cond_bi", "L0_cond_Wo", "L0_cond_bo",
        "L0_cond_gamma", "L0_cond_beta"]


def kernel(**inputs):
    import numpy as _np
    import concourse.bacc as _bacc
    from concourse import mybir as _mybir
    from concourse.bass_utils import run_bass_kernel_spmd as _run

    nc = _bacc.Bacc("TRN2", target_bir_lowering=False, num_devices=1)
    arrays, args = {}, []
    for name in _INS:
        a = _np.ascontiguousarray(inputs[name])
        arrays[f"in_{name}_dram"] = a
        args.append(nc.dram_tensor(f"in_{name}_dram", a.shape, _mybir.dt.from_np(a.dtype), kind="ExternalInput").ap())
    x = arrays["in_x_dram"]
    out = nc.dram_tensor("out_0_dram", x.shape, _mybir.dt.float32, kind="ExternalOutput").ap()
    build_ffn_norm_rotate(nc, *args, out)
    r = _run(nc, [arrays], core_ids=[0])
    return r.results[0]["out_0_dram"]
```
